# Optimizing a Trainium2 kernel written in Bass

```python
import numpy as np
import jax
import jax.numpy as jnp

def _softmax(x, axis=-1):
    return jax.nn.softmax(x, axis=axis)

def _gelu(x):
    return jax.nn.gelu(x, approximate=True)

def _silu(x):
    return jax.nn.silu(x)

def _sigmoid(x):
    return jax.nn.sigmoid(x)

def _layernorm(x, axis=-1, eps=1e-05):
    m = jnp.mean(x, axis=axis, keepdims=True)
    v = jnp.var(x, axis=axis, keepdims=True)
    return (x - m) / jnp.sqrt(v + eps)

def _scatter_add(tgt, idx, src, axis=0):
    return tgt.at[idx].add(src)

def _segment_sum(src, seg, n):
    return jax.ops.segment_sum(src, seg, n)
kernel_name = 'mk_conv_seq_d1_conv_nchw384_r4_a9dfc2'

def setup_inputs(seed: int=0):
    np.random.seed(seed)
    _w = jnp.asarray

    def _rec_inputs():
        import jax
        import jax.numpy as jnp
        _gk = jax.random.key(seed)
        x = -0.0001476 + 0.9999 * jax.random.normal(jax.random.fold_in(_gk, 1), (32, 96, 56, 56), jnp.float32)
        return x
    x = _rec_inputs()

    def _L0_conv_setup():
        import jax, jax.numpy as jnp
        import numpy as np
        WS = 7
        SS = 3
        NH = 12
        EPS = 1e-05

        def _build_mask(H, W):
            img = np.zeros((H, W), dtype=np.float32)
            cnt = 0
            sl = (slice(0, -WS), slice(-WS, -SS), slice(-SS, None))
            for hs in sl:
                for ws in sl:
                    img[hs, ws] = cnt
                    cnt += 1
            mw = img.reshape(H // WS, WS, W // WS, WS).transpose(0, 2, 1, 3).reshape(-1, WS * WS)
            diff = mw[:, None, :] - mw[:, :, None]
            return jnp.asarray(np.where(diff != 0, -100.0, 0.0).astype(np.float32))

        def _ln(x, g, b):
            m = jnp.mean(x, axis=-1, keepdims=True)
            v = jnp.mean(jnp.square(x - m), axis=-1, keepdims=True)
            return (x - m) * jax.lax.rsqrt(v + EPS) * g + b

        def _window_partition(x):
            B, H, W, C = x.shape
            x = x.reshape(B, H // WS, WS, W // WS, WS, C)
            return x.transpose(0, 1, 3, 2, 4, 5).reshape(-1, WS * WS, C)

        def _window_reverse(w, H, W, B):
            C = w.shape[-1]
            x = w.reshape(B, H // WS, W // WS, WS, WS, C)
            return x.transpose(0, 1, 3, 2, 4, 5).reshape(B, H, W, C)
        key = jax.random.key(seed)
        ks = jax.random.split(key, 8)
        C, R = (96, 2.0)
        Hd = int(C * R)
        s = 0.02
        return {'x': jax.random.normal(ks[0], (32, C, 56, 56), dtype=jnp.float32), 'g1': jnp.ones((C,), jnp.float32), 'b1': jnp.zeros((C,), jnp.float32), 'w_qkv': s * jax.random.normal(ks[1], (C, 3 * C), jnp.float32), 'b_qkv': jnp.zeros((3 * C,), jnp.float32), 'w_proj': s * jax.random.normal(ks[2], (C, C), jnp.float32), 'b_proj': jnp.zeros((C,), jnp.float32), 'g2': jnp.ones((C,), jnp.float32), 'b2': jnp.zeros((C,), jnp.float32), 'w_fc1': s * jax.random.normal(ks[3], (C, Hd), jnp.float32), 'b_fc1': jnp.zeros((Hd,), jnp.float32), 'w_fc2': s * jax.random.normal(ks[4], (Hd, C), jnp.float32), 'b_fc2': jnp.zeros((C,), jnp.float32)}
    _L0_conv_all = _L0_conv_setup()
    _L0_conv_in = {k: v for k, v in _L0_conv_all.items() if k in ('g1', 'b1', 'w_qkv', 'b_qkv', 'w_proj', 'b_proj', 'g2', 'b2', 'w_fc1', 'b_fc1', 'w_fc2', 'b_fc2')}
    del _L0_conv_all
    return {'x': x, 'L0_conv_g1': _L0_conv_in['g1'], 'L0_conv_b1': _L0_conv_in['b1'], 'L0_conv_w_qkv': _L0_conv_in['w_qkv'], 'L0_conv_b_qkv': _L0_conv_in['b_qkv'], 'L0_conv_w_proj': _L0_conv_in['w_proj'], 'L0_conv_b_proj': _L0_conv_in['b_proj'], 'L0_conv_g2': _L0_conv_in['g2'], 'L0_conv_b2': _L0_conv_in['b2'], 'L0_conv_w_fc1': _L0_conv_in['w_fc1'], 'L0_conv_b_fc1': _L0_conv_in['b_fc1'], 'L0_conv_w_fc2': _L0_conv_in['w_fc2'], 'L0_conv_b_fc2': _L0_conv_in['b_fc2']}

def reference(x, L0_conv_g1, L0_conv_b1, L0_conv_w_qkv, L0_conv_b_qkv, L0_conv_w_proj, L0_conv_b_proj, L0_conv_g2, L0_conv_b2, L0_conv_w_fc1, L0_conv_b_fc1, L0_conv_w_fc2, L0_conv_b_fc2):
    import jax
    import jax.numpy as jnp

    def _L0_conv_ref(x, g1, b1, w_qkv, b_qkv, w_proj, b_proj, g2, b2, w_fc1, b_fc1, w_fc2, b_fc2):
        import jax, jax.numpy as jnp
        import numpy as np
        WS = 7
        SS = 3
        NH = 12
        EPS = 1e-05

        def _build_mask(H, W):
            img = np.zeros((H, W), dtype=np.float32)
            cnt = 0
            sl = (slice(0, -WS), slice(-WS, -SS), slice(-SS, None))
            for hs in sl:
                for ws in sl:
                    img[hs, ws] = cnt
                    cnt += 1
            mw = img.reshape(H // WS, WS, W // WS, WS).transpose(0, 2, 1, 3).reshape(-1, WS * WS)
            diff = mw[:, None, :] - mw[:, :, None]
            return jnp.asarray(np.where(diff != 0, -100.0, 0.0).astype(np.float32))

        def _ln(x, g, b):
            m = jnp.mean(x, axis=-1, keepdims=True)
            v = jnp.mean(jnp.square(x - m), axis=-1, keepdims=True)
            return (x - m) * jax.lax.rsqrt(v + EPS) * g + b

        def _window_partition(x):
            B, H, W, C = x.shape
            x = x.reshape(B, H // WS, WS, W // WS, WS, C)
            return x.transpose(0, 1, 3, 2, 4, 5).reshape(-1, WS * WS, C)

        def _window_reverse(w, H, W, B):
            C = w.shape[-1]
            x = w.reshape(B, H // WS, W // WS, WS, WS, C)
            return x.transpose(0, 1, 3, 2, 4, 5).reshape(B, H, W, C)
        B, C, H, W = x.shape
        hd = C // NH
        scale = hd ** (-0.5)
        L = WS * WS
        nW = H // WS * (W // WS)
        residual = x
        f = x.transpose(0, 2, 3, 1)
        f = _ln(f, g1, b1)
        f = jnp.roll(f, (-SS, -SS), axis=(1, 2))
        win = _window_partition(f)
        qkv = win @ w_qkv + b_qkv
        qkv = qkv.reshape(-1, L, 3, NH, hd).transpose(2, 0, 3, 1, 4)
        q, k, v = (qkv[0], qkv[1], qkv[2])
        attn = jnp.einsum('bhid,bhjd->bhij', q, k) * scale
        mask = _build_mask(H, W)
        attn = attn.reshape(B, nW, NH, L, L) + mask[None, :, None]
        attn = jax.nn.softmax(attn.reshape(-1, NH, L, L), axis=-1)
        out = jnp.einsum('bhij,bhjd->bihd', attn, v).reshape(-1, L, C)
        out = out @ w_proj + b_proj
        f = _window_reverse(out, H, W, B)
        f = jnp.roll(f, (SS, SS), axis=(1, 2))
        f = residual + f.transpose(0, 3, 1, 2)
        m = _ln(f.transpose(0, 2, 3, 1), g2, b2)
        m = jax.nn.gelu(m @ w_fc1 + b_fc1, approximate=False) @ w_fc2 + b_fc2
        return f + m.transpose(0, 3, 1, 2)

    def _gn(v, G=32, eps=1e-05):
        B_, C_, H_, W_ = v.shape
        g = v.reshape(B_, G, C_ // G, H_, W_)
        m = jnp.mean(g, axis=(2, 3, 4), keepdims=True)
        s = jnp.var(g, axis=(2, 3, 4), keepdims=True)
        return ((g - m) / jnp.sqrt(s + eps)).reshape(v.shape)

    def _ln_c(v, eps=1e-06):
        m = jnp.mean(v, axis=1, keepdims=True)
        s = jnp.var(v, axis=1, keepdims=True)
        return (v - m) / jnp.sqrt(s + eps)

    def _ln_t(v, eps=1e-05):
        m = jnp.mean(v, axis=-1, keepdims=True)
        s = jnp.var(v, axis=-1, keepdims=True)
        return (v - m) / jnp.sqrt(s + eps)

    def _to_tokens(v):
        B_, C_, H_, W_ = v.shape
        return v.reshape(B_, C_, H_ * W_).transpose(0, 2, 1)

    def _from_tokens(t, like):
        B_, C_, H_, W_ = like.shape
        return t.transpose(0, 2, 1).reshape(B_, C_, H_, W_)
    x = _L0_conv_ref(x, L0_conv_g1, L0_conv_b1, L0_conv_w_qkv, L0_conv_b_qkv, L0_conv_w_proj, L0_conv_b_proj, L0_conv_g2, L0_conv_b2, L0_conv_w_fc1, L0_conv_b_fc1, L0_conv_w_fc2, L0_conv_b_fc2)
    return x

_drawn_inputs = setup_inputs


def setup_inputs(seed=0):
    import zlib

    import numpy as np

    out = dict(_drawn_inputs(seed))
    spreads = {'L0_conv_g1': (1.0, 0.6),
     'L0_conv_b1': (0.0, 0.8),
     'L0_conv_b_qkv': (0.0, 0.454),
     'L0_conv_b_proj': (0.0, 0.1),
     'L0_conv_g2': (1.0, 0.6),
     'L0_conv_b2': (0.0, 2.0),
     'L0_conv_b_fc1': (0.0, 0.597),
     'L0_conv_b_fc2': (0.0, 0.1)}
    factors = {'L0_conv_w_qkv': 7.016, 'L0_conv_w_proj': 2.993}
    for name, (base, spread) in spreads.items():
        noise = np.random.default_rng([zlib.crc32(name.encode()), seed]).standard_normal(out[name].shape)
        drawn = base * np.exp(spread * noise) if base else spread * noise
        out[name] = jnp.asarray(drawn.astype(out[name].dtype))
    for name, factor in factors.items():
        out[name] = (out[name] * factor).astype(out[name].dtype)
    return out
```

```python
from contextlib import ExitStack

import numpy as np
import concourse.bass as bass
import concourse.mybir as mybir

F32 = mybir.dt.float32
F16 = mybir.dt.float16
ALU = mybir.AluOpType
ACT = mybir.ActivationFunctionType
AX = mybir.AxisListType

C, SIDE, WS, SHIFT, NH = 96, 56, 7, 3, 12
HD = C // NH
L = WS * WS
BANDS = SIDE // WS
PAIRS = BANDS // 2
TOK = BANDS * L
PT = 2 * L
W1 = 64
PR = W1 + L
QUADS = NH // 4
HID = 2 * C
SR = 3 * 32
MASK0, MAX0, ROWS = SR, SR + 4, SR + 8
UNITS = PAIRS * QUADS // 2
CH = 4 * L
EPS = 1e-5
SCALE = HD ** -0.5

LOAD, ORDER, TOKENS, QK, STACK, SCORE, MAXIMA, PROB, PROJ, MLP = 7, 6, 5, 4, 3, 2, 1, 0, -1, -2
GENERAL = {"ot": PROJ, "mt": MAXIMA, "t2": QK, "t1": TOKENS, "proj": PROJ, "nt2": MLP, "q": QK, "k": QK,
           "fca": MLP, "fcb": MLP, "v": STACK, "nt1": PROJ, "fc2": MLP}
ORDERED = list(GENERAL)
TAKES = {name: 2 if name == "v" else 1 for name in ORDERED}
N_CONST = 7 + 11 + 8


class Band:

    def __init__(self, i, c):
        self.i, self.c = i, c

    def count(self, per, add=0):
        return per * self.c + add if self.i is None else self.i * (BANDS * per) + (per * self.c + add)

    def used(self, ring, per):
        fixed = (self.c // ring + 1) * per
        return fixed if self.i is None else self.i * (BANDS // ring * per) + fixed

    def image(self):
        return self.c // BANDS if self.i is None else self.i + self.c // BANDS

    def step(self, d):
        return Band(self.i, self.c + d)


def build(nc, x, g1, b1, wqkv, bqkv, wproj, bproj, g2, b2, wfc1, bfc1, wfc2, bfc2,
          ident_d, heads_d, rows_d, out):
    images = x.shape[0]
    NB = images * BANDS
    FIRST = 3 - MLP
    rounds = images - 2

    ctx = ExitStack()
    with ctx:
        def sb(name, shape, dt=F32):
            return ctx.enter_context(nc.sbuf_tensor(name, shape, dt))

        def sem(name):
            return ctx.enter_context(nc.semaphore(name))

        ident = sb("ident", [128, 128])
        heads = sb("heads", [ROWS, 8])
        wraw, w1raw = sb("wraw", [C, 3 * C]), sb("w1raw", [C, HID])
        wq, wk, wv, wp = sb("wq", [C, C]), sb("wk", [C, C]), sb("wv", [C, C]), sb("wp", [C, C])
        w1, w2 = sb("w1", [C, HID]), sb("w2", [C, 2, C])
        vec = sb("vec", [C, 11])
        G1, B1, BQ, BK, BV, BP, G2, B2, BF1, BF2 = 0, 1, 2, 3, 4, 5, 6, 7, 8, 10
        bias = sb("bias", [C, 6])
        half = sb("half", [128, PAIRS])
        xr = sb("xr", [C, 4, WS, SIDE])
        xw = sb("xw", [C, 8, TOK])
        tok1, tok2 = sb("tok1", [PT, 2, PAIRS, C]), sb("tok2", [PT, 2, PAIRS, C])
        st1, st2 = sb("st1", [PT, 2, PAIRS, 6]), sb("st2", [PT, 2, PAIRS, 6])
        mv1, mv2 = sb("mv1", [PT, 2, PAIRS, 2]), sb("mv2", [PT, 2, PAIRS, 2])
        ve1, ve2 = sb("ve1", [PT, 2, PAIRS]), sb("ve2", [PT, 2, PAIRS])
        rs1, rs2 = sb("rs1", [PT, 2, PAIRS]), sb("rs2", [PT, 2, PAIRS])
        xn1, xn2 = sb("xn1", [PT, 2, PAIRS, C]), sb("xn2", [PT, 2, PAIRS, C])
        xnT, fnT = sb("xnT", [C, 2, TOK]), sb("fnT", [C, 2, TOK])
        nat = sb("nat", [C, 2, 4, TOK], F16)
        qst = sb("qst", [ROWS, 4, QUADS, TOK], F16)
        kst = sb("kst", [ROWS, 4, QUADS, TOK], F16)
        qbd = sb("qbd", [ROWS, 2, QUADS, 4, TOK], F16)
        kbd = sb("kbd", [ROWS, 2, QUADS, 4, TOK], F16)
        vbd = sb("vbd", [PR, 4, PAIRS * NH, 2, HD + 1])
        nmax = sb("nmax", [PR, 2, PAIRS * NH])
        mrow = sb("mrow", [PAIRS * NH, 2, PT], F16)
        probs = sb("probs", [PR, 2, PAIRS * QUADS, CH])
        rsum = sb("rsum", [L, 2, PAIRS * NH])
        on = sb("on", [L, 2, PAIRS * 2, C])
        oT = sb("oT", [C, 2, TOK])
        f, fb = sb("f", [C, 4, TOK]), sb("fb", [C, 4, TOK])
        hid = sb("hid", [C, 2, 2, TOK])
        yr = sb("yr", [C, 2, WS, SIDE])

        psum = ctx.enter_context(nc.psum_tensor("psum", [128, 8, 512], F32))
        S_BANK, P_BANK, O_BANK, G_BANK = 0, 2, 4, 6

        nat_d = nc.dram_tensor("nat_d", [2, C, 4, TOK], F16, kind="Internal").ap()
        max_d = nc.dram_tensor("max_d", [2, PAIRS, NH, PT], F16, kind="Internal").ap()

        consts_in, vbd_zero, vbd_ones = sem("consts_in"), sem("vbd_zero"), sem("vbd_ones")
        psum_clear, weights_set = sem("psum_clear"), sem("weights_set")
        bias_made, bias_set = sem("bias_made"), sem("bias_set")
        x_in = [sem(f"x_in{n}") for n in range(4)]
        nat_out = [sem(f"nat_out{n}") for n in range(2)]
        stack_in = [sem(f"stack_in{n}") for n in range(4)]
        max_out = [sem(f"max_out{n}") for n in range(2)]
        max_in = [sem(f"max_in{n}") for n in range(2)]
        y_out = [sem(f"y_out{n}") for n in range(2)]
        STACK_IN = [6 * 16, 6 * 16, 6 * 16, 8 * 16]
        made = {name: sem(f"made_{name}") for name in ORDERED}
        taken = {name: sem(f"taken_{name}") for name in ORDERED}
        passed = sem("passed")
        x_ordered, f_biased = sem("x_ordered"), sem("f_biased")
        bn1, stats1, eps1, root1, normed1 = (sem(n) for n in ("bn1", "stats1", "eps1", "root1", "normed1"))
        bn2, stats2, eps2, root2, normed2 = (sem(n) for n in ("bn2", "stats2", "eps2", "root2", "normed2"))
        q_hi, k_hi = sem("q_hi"), sem("k_hi")
        k_blocks, q_blocks = sem("k_blocks"), sem("q_blocks")
        s_made, s_maxed = sem("s_made"), sem("s_maxed")
        p_made, exp_done = sem("p_made"), sem("exp_done")
        pv_made, o_inverted, o_normed = sem("pv_made"), sem("o_inverted"), sem("o_normed")

        block = ctx.enter_context(nc.Block())

        def steps(engine, step):
            for t in range(-LOAD, FIRST):
                step(Band(None, t))
            with engine.Fori(0, rounds) as i:
                for t in range(BANDS):
                    step(Band(i, FIRST + t))
            for t in range(FIRST + BANDS * rounds, NB - MLP):
                step(Band(None, t))

        def has(b):
            return b.i is not None or 0 <= b.c < NB

        def wait(engine, s, value):
            if not isinstance(value, int) or value > 0:
                engine.wait_ge(s, value)

        def alone(engine):
            engine.sem_inc(passed, 1)

        def bank(t, name):
            return G_BANK + (t.c * len(ORDERED) + ORDERED.index(name)) % 2

        def chunk(u, n):
            return divmod(2 * u + n, QUADS)

        def image_rows(c):
            r = (c % BANDS) * WS + SHIFT
            return [(0, r, WS - SHIFT), (WS - SHIFT, (r + WS - SHIFT) % SIDE, SHIFT)]

        @block.sync
        def _(sp):
            def const(dst, src):
                sp.dma_start(dst, src).then_inc(consts_in, 16)

            def column(n, v):
                const(vec[:, n:n + 1], v.rearrange("(c a) -> c a", a=1))

            const(ident[:, :], ident_d)
            const(heads[:, :], heads_d)
            const(wraw[:, :], wqkv)
            const(w1raw[:, :], wfc1)
            const(wp[:, :], wproj)
            for m in range(2):
                const(w2[:, m, :], wfc2[m * C:(m + 1) * C, :])
                column(BF1 + m, bfc1[m * C:(m + 1) * C])
            for m in range(3):
                column(BQ + m, bqkv[m * C:(m + 1) * C])
            for n, v in ((G1, g1), (B1, b1), (BP, bproj), (G2, g2), (B2, b2), (BF2, bfc2)):
                column(n, v)
            for n in range(4):
                const(qst[MASK0:ROWS, n, :, :], rows_d[0, 0, :, :, :])
                const(kst[MASK0:ROWS, n, :, :], rows_d[1, 0, :, :, :])
            sp.wait_ge(consts_in, 16 * N_CONST)

            def load_x(b):
                n = b.c % 4
                wait(sp, x_ordered, b.count(1, -3))
                alone(sp)
                for at, row, rows in image_rows(b.c):
                    sp.dma_start(xr[:, n, at:at + rows, :], x[b.image(), :, row:row + rows, :]).then_inc(x_in[n], 16)

            def stacks(b):
                n = b.c % 4
                wait(sp, p_made, b.count(UNITS, -3 * UNITS))
                alone(sp)
                if n == 3:
                    kind = int(b.c % BANDS == BANDS - 1)
                    sp.dma_start(qst[MASK0:MAX0, n, :, :], rows_d[0, kind, 0:4, :, :]).then_inc(stack_in[n], 16)
                    sp.dma_start(kst[MASK0:MAX0, n, :, :], rows_d[1, kind, 0:4, :, :]).then_inc(stack_in[n], 16)
                sp.wait_ge(nat_out[b.c % 2], b.used(2, 16))
                alone(sp)
                src = nat_d[b.c % 2, :, :, :].rearrange("(c r) n t -> n r c t", c=QUADS)
                for stack, parts in ((kst, (2, 3, 2)), (qst, (0, 0, 1))):
                    for m, part in enumerate(parts):
                        sp.dma_start(stack[32 * m:32 * m + 32, n, :, :], src[part, :, :, :]).then_inc(stack_in[n], 16)

            def maxima(b):
                n = b.c % 2
                wait(sp, max_in[n], b.step(-2).used(2, QUADS * 16))
                alone(sp)
                sp.wait_ge(taken["mt"], b.count(1, 1))
                alone(sp)
                sp.dma_start(max_d[n, :, :, :].rearrange("p h t -> (p h) t"), mrow[:, n, :]).then_inc(max_out[n], 16)
                sp.wait_ge(max_out[n], b.used(2, 16))
                alone(sp)
                for c in range(QUADS):
                    sp.dma_start(qst[MAX0:ROWS, b.c % 4, c, :].rearrange("h (p t) -> h p t", t=PT),
                                 max_d[n, :, 4 * c:4 * c + 4, :].rearrange("p h t -> h p t")).then_inc(max_in[n], 16)

            def save_parts(b):
                n = b.c % 2
                wait(sp, stack_in[(b.c - 2) % 4], b.step(-2).used(4, STACK_IN[(b.c - 2) % 4]))
                alone(sp)
                sp.wait_ge(taken["q"], b.count(1, 1))
                alone(sp)
                sp.wait_ge(taken["k"], b.count(1, 1))
                alone(sp)
                sp.dma_start(nat_d[n, :, :, :], nat[:, n, :, :]).then_inc(nat_out[n], 16)

            def store_y(b):
                n = b.c % 2
                sp.wait_ge(taken["fc2"], b.count(1, 1))
                alone(sp)
                for at, row, rows in image_rows(b.c):
                    sp.dma_start(out[b.image(), :, row:row + rows, :], yr[:, n, at:at + rows, :]).then_inc(y_out[n], 16)

            def step(t):
                for offset, stage in ((LOAD, load_x), (STACK, stacks), (MAXIMA, maxima), (QK, save_parts), (MLP, store_y)):
                    if has(t.step(offset)):
                        stage(t.step(offset))

            steps(sp, step)
            for n in range(2):
                sp.wait_ge(y_out[n], 2 * 16 * NB // 2)

        @block.gpsimd
        def _(pool):
            nc.gpsimd.memset(half[:, :], -0.5)
            nc.gpsimd.memset(vbd[:, :, :, :, :], 0.0).then_inc(vbd_zero, 1)
            pool.wait_ge(vbd_zero, 1)
            nc.gpsimd.memset(vbd[0:L, :, :, 0, HD:HD + 1], 1.0)
            nc.gpsimd.memset(vbd[W1:PR, :, :, 1, HD:HD + 1], 1.0).then_inc(vbd_ones, 1)
            pool.wait_ge(vbd_ones, 1)
            pool.wait_ge(consts_in, 16 * N_CONST)

            def order_x(b):
                pool.wait_ge(x_in[b.c % 4], b.used(4, 2 * 16))
                alone(pool)
                wait(pool, taken["proj"], b.count(1, -7))
                alone(pool)
                src, dst, inner = xr[:, b.c % 4, :, :], xw[:, b.c % 8, :], BANDS - 1
                nc.gpsimd.tensor_copy(dst[:, 0:inner * L].rearrange("c (w r s) -> c w r s", w=inner, r=WS),
                                      src[:, :, SHIFT:SHIFT + inner * WS].rearrange("c r (w s) -> c w r s", s=WS))
                end = dst[:, inner * L:TOK].rearrange("c (r s) -> c r s", r=WS)
                nc.gpsimd.tensor_copy(end[:, :, 0:WS - SHIFT], src[:, :, SIDE - WS + SHIFT:SIDE])
                nc.gpsimd.tensor_copy(end[:, :, WS - SHIFT:WS], src[:, :, 0:SHIFT]).then_inc(x_ordered, 1)

            def add_bias(b):
                n = b.c % 4
                pool.wait_ge(taken["proj"], b.count(1, 1))
                alone(pool)
                wait(pool, taken["fc2"], b.count(1, -3))
                alone(pool)
                nc.gpsimd.tensor_scalar(fb[:, n, :], f[:, n, :], vec[:, BF2:BF2 + 1], None, ALU.add).then_inc(f_biased, 1)

            def root(b, mv, ve, rs, stats, eps, done):
                n = b.c % 2
                pool.wait_ge(stats, b.count(1, 1))
                alone(pool)
                nc.gpsimd.tensor_scalar(ve[:, n, :], mv[:, n, :, 1], EPS, None, ALU.add).then_inc(eps, 1)
                pool.wait_ge(eps, b.count(1, 1))
                alone(pool)
                nc.gpsimd.tensor_tensor(rs[:, n, :], ve[:, n, :], half[0:PT, :], ALU.pow).then_inc(done, 1)

            def step(t):
                if has(t.step(ORDER)):
                    order_x(t.step(ORDER))
                if has(t.step(PROJ)):
                    add_bias(t.step(PROJ))
                if has(t.step(TOKENS)):
                    root(t.step(TOKENS), mv1, ve1, rs1, stats1, eps1, root1)
                if has(t.step(PROJ)):
                    root(t.step(PROJ), mv2, ve2, rs2, stats2, eps2, root2)

            steps(pool, step)

        @block.tensor
        def _(pe):
            pe.wait_ge(consts_in, 16 * N_CONST)
            pe.wait_ge(psum_clear, 1)
            for n in range(3):
                nc.tensor.matmul(psum[0:C, 0, n:n + 1], wraw[:, n * C:(n + 1) * C], vec[:, B1:B1 + 1], start=True, stop=True)
            for n in range(2):
                last = nc.tensor.matmul(psum[0:C, 0, 3 + n:4 + n], w1raw[:, n * C:(n + 1) * C], vec[:, B2:B2 + 1], start=True, stop=True)
            last.then_inc(bias_made, 1)
            pe.wait_ge(bias_set, 1)
            nc.tensor.matmul(psum[0:C, 0, 5:6], wp[:, :], bias[:, 2:3], start=True, stop=True).then_inc(bias_made, 1)
            pe.wait_ge(bias_set, 2)
            pe.wait_ge(weights_set, 1)
            pe.wait_ge(vbd_ones, 1)

            def general(t, name):
                at = t.c * len(ORDERED) + ORDERED.index(name) - 2
                while True:
                    c, n = divmod(at, len(ORDERED))
                    before = Band(t.i, c + GENERAL[ORDERED[n]])
                    if has(before):
                        per = TAKES[ORDERED[n]]
                        pe.wait_ge(taken[ORDERED[n]], before.count(per, per))
                        break
                    at -= 2
                    if at < -LOAD * len(ORDERED):
                        break
                return psum[:, bank(t, name), :]

            def transposes(t, name, ready, src, rows):
                b = t.step(GENERAL[name])
                if not has(b):
                    return
                pe.wait_ge(ready, b.count(1, 1))
                dst = general(t, name)
                for p in range(PAIRS):
                    part = src(b, p)
                    other = PT + C - rows
                    last = nc.tensor.transpose(dst[0:other, p * rows:(p + 1) * rows], part, ident[0:rows, 0:rows])
                last.then_inc(made[name], 1)

            def dense(t, name, ready, parts):
                b = t.step(GENERAL[name])
                if not has(b):
                    return
                pe.wait_ge(ready, b.count(1, 1))
                dst = general(t, name)
                parts = parts(b)
                for n, (weights, tokens) in enumerate(parts):
                    last = nc.tensor.matmul(dst[0:C, 0:TOK], weights, tokens, start=n == 0, stop=n == len(parts) - 1)
                last.then_inc(made[name], 1)

            def values(t):
                b = t.step(STACK)
                if not has(b):
                    return
                dst = general(t, "v")
                for p in range(PAIRS):
                    for w in range(2):
                        at = (2 * p + w) * L
                        last = nc.tensor.matmul(dst[W1 * w:W1 * w + L, p * C:(p + 1) * C], xnT[:, b.c % 2, at:at + L], wv[:, :], start=True, stop=True)
                last.then_inc(made["v"], 1)

            def out_transposes(t):
                b = t.step(PROJ)
                if not has(b):
                    return
                pe.wait_ge(o_normed, b.count(2, 2))
                dst = general(t, "ot")
                alone(pe)
                for p in range(PAIRS):
                    for w in range(2):
                        at = (2 * p + w) * L
                        last = nc.tensor.transpose(dst[0:C, at:at + L], on[:, b.c % 2, 2 * p + w, :], ident[0:L, 0:L])
                last.then_inc(made["ot"], 1)

            def max_transpose(t):
                b = t.step(MAXIMA)
                if not has(b):
                    return
                pe.wait_ge(s_maxed, b.count(UNITS, UNITS))
                dst = general(t, "mt")
                alone(pe)
                nc.tensor.transpose(dst[0:PAIRS * NH, 0:PR], nmax[:, b.c % 2, :], ident[0:PR, 0:PR]).then_inc(made["mt"], 1)

            def score_bank(b, u, first_bank, side, blocks, done):
                for n in range(2):
                    p, c = chunk(u, n)
                    for w in range(2):
                        at = (2 * p + w) * L
                        last = nc.tensor.matmul(psum[W1 * w:W1 * w + L, first_bank + u % 2, n * CH:(n + 1) * CH],
                                                side[:, b.c % 4, c, at:at + L], blocks[:, b.c % 2, c, :, at:at + L], start=True, stop=True)
                last.then_inc(done, 1)

            def scores(t, u):
                b = t.step(SCORE)
                if has(b):
                    if u == 0:
                        pe.wait_ge(k_blocks, b.count(1, 1))
                    wait(pe, s_maxed, b.count(UNITS, u - 1))
                    score_bank(b, u, S_BANK, qst, kbd, s_made)

            def shifted(t, u):
                b = t.step(PROB)
                if has(b):
                    if u == 0:
                        pe.wait_ge(q_blocks, b.count(1, 1))
                    wait(pe, exp_done, b.count(UNITS, u - 1))
                    score_bank(b, u, P_BANK, kst, qbd, p_made)

            def weighted(t, p):
                b = t.step(PROB)
                if not has(b):
                    return
                if p == 0:
                    pe.wait_ge(taken["v"], b.count(2, 2))
                pe.wait_ge(exp_done, b.count(UNITS, (QUADS * p + QUADS - 1) // 2 + 1))
                if p % 2 == 0:
                    wait(pe, o_normed, b.count(2, p // 2 - 1))
                dst = psum[0:L, O_BANK + p // 2, 0:2 * 2 * NH * (HD + 1)].rearrange("t (p w h e) -> t p w h e", p=2, w=2, h=NH)
                for h in range(NH):
                    last = nc.tensor.matmul(dst[:, p % 2, :, h, :],
                                            probs[:, b.c % 2, p * QUADS + h // 4, h % 4 * L:(h % 4 + 1) * L],
                                            vbd[:, b.c % 4, p * NH + h, :, :], start=True, stop=True)
                if p % 2:
                    last.then_inc(pv_made, 1)

            def step(t):
                shifted(t, 0)
                scores(t, 0)
                out_transposes(t)
                max_transpose(t)
                shifted(t, 1)
                scores(t, 1)
                transposes(t, "t2", normed1, lambda b, p: xn1[:, b.c % 2, p, :], PT)
                transposes(t, "t1", x_ordered, lambda b, p: xw[:, b.c % 8, p * PT:(p + 1) * PT], C)
                weighted(t, 0)
                dense(t, "proj", taken["ot"], lambda b: [(wp[:, :], oT[:, b.c % 2, :])])
                transposes(t, "nt2", normed2, lambda b, p: xn2[:, b.c % 2, p, :], PT)
                shifted(t, 2)
                scores(t, 2)
                dense(t, "q", taken["t2"], lambda b: [(wq[:, :], xnT[:, b.c % 2, :])])
                dense(t, "k", taken["t2"], lambda b: [(wk[:, :], xnT[:, b.c % 2, :])])
                weighted(t, 1)
                dense(t, "fca", taken["nt2"], lambda b: [(w1[:, 0:C], fnT[:, b.c % 2, :])])
                dense(t, "fcb", taken["nt2"], lambda b: [(w1[:, C:HID], fnT[:, b.c % 2, :])])
                shifted(t, 3)
                scores(t, 3)
                values(t)
                shifted(t, 4)
                scores(t, 4)
                weighted(t, 2)
                transposes(t, "nt1", taken["proj"], lambda b, p: f[:, b.c % 4, p * PT:(p + 1) * PT], C)
                shifted(t, 5)
                scores(t, 5)
                dense(t, "fc2", taken["fcb"], lambda b: [(w2[:, m, :], hid[:, b.c % 2, m, :]) for m in range(2)])
                weighted(t, 3)

            steps(pe, step)

        @block.scalar
        def _(act):
            act.wait_ge(bias_set, 2)
            act.wait_ge(vbd_ones, 1)

            def product(t, name):
                b = t.step(GENERAL[name])
                act.wait_ge(made[name], b.count(1, 1))
                return b, psum[:, bank(t, name), :]

            def out_by_channel(t):
                b, src = product(t, "ot")
                wait(act, made["proj"], b.count(1, -1))
                nc.scalar.activation(oT[:, b.c % 2, :], src[0:C, 0:TOK], ACT.Copy).then_inc(taken["ot"], 1)

            def max_rows(t):
                b, src = product(t, "mt")
                wait(act, max_out[b.c % 2], b.step(-2).used(2, 16))
                nc.scalar.activation(mrow[:, b.c % 2, :].rearrange("h (w t) -> h w t", w=2),
                                     src[0:PAIRS * NH, 0:2 * W1].rearrange("h (w t) -> h w t", w=2)[:, :, 0:L],
                                     ACT.Copy).then_inc(taken["mt"], 1)

            def x_by_channel(t):
                b, src = product(t, "t2")
                wait(act, made["v"], b.count(1, -1))
                nc.scalar.activation(xnT[:, b.c % 2, :], src[0:C, 0:TOK], ACT.Copy).then_inc(taken["t2"], 1)

            def x_by_token(t):
                b, src = product(t, "t1")
                wait(act, normed1, b.count(1, -1))
                nc.scalar.activation(tok1[:, b.c % 2, :, :], src[0:PT, 0:PAIRS * C].rearrange("t (p c) -> t p c", c=C), ACT.Copy).then_inc(taken["t1"], 1)

            def f_by_channel(t):
                b, src = product(t, "nt2")
                wait(act, made["fcb"], b.count(1, -1))
                nc.scalar.activation(fnT[:, b.c % 2, :], src[0:C, 0:TOK], ACT.Copy).then_inc(taken["nt2"], 1)

            def f_by_token(t):
                b, src = product(t, "nt1")
                wait(act, normed2, b.count(1, -1))
                nc.scalar.activation(tok2[:, b.c % 2, :, :], src[0:PT, 0:PAIRS * C].rearrange("t (p c) -> t p c", c=C), ACT.Copy).then_inc(taken["nt1"], 1)

            def high_part(t, name, part, col, done):
                b, src = product(t, name)
                if name == "q":
                    wait(act, nat_out[b.c % 2], b.step(-2).used(2, 16))
                nc.scalar.activation(nat[:, b.c % 2, part, :], src[0:C, 0:TOK], ACT.Identity, bias=bias[:, col:col + 1]).then_inc(done, 1)

            def value_blocks(t):
                b, src = product(t, "v")
                wait(act, pv_made, b.count(2, -6))
                for w in range(2):
                    rows = slice(W1 * w, W1 * w + L)
                    nc.scalar.activation(vbd[rows, b.c % 4, :, w, 0:HD], src[rows, 0:PAIRS * C].rearrange("t (h d) -> t h d", d=HD),
                                         ACT.Copy).then_inc(taken["v"], 1)

            def exps(t, u):
                b = t.step(PROB)
                if has(b):
                    act.wait_ge(p_made, b.count(UNITS, u + 1))
                    if u == 0:
                        wait(act, pv_made, b.count(2, -2))
                    nc.scalar.activation(probs[:, b.c % 2, 2 * u:2 * u + 2, :], psum[0:PR, P_BANK + u % 2, 0:2 * CH].rearrange("j (n k) -> j n k", n=2),
                                         ACT.Exp).then_inc(exp_done, 1)

            def gelu(t, name, m):
                b, src = product(t, name)
                if m == 0:
                    wait(act, made["fc2"], b.count(1, -1))
                nc.scalar.activation(hid[:, b.c % 2, m, :], src[0:C, 0:TOK], ACT.Gelu, bias=bias[:, 3 + m:4 + m]).then_inc(taken[name], 1)

            def step(t):
                def run(offset, stage, *more):
                    if has(t.step(offset)):
                        stage(t, *more)

                exps(t, 0)
                run(PROJ, out_by_channel)
                run(MAXIMA, max_rows)
                exps(t, 1)
                run(QK, x_by_channel)
                run(TOKENS, x_by_token)
                run(MLP, f_by_channel)
                exps(t, 2)
                run(QK, high_part, "q", 0, 0, q_hi)
                run(QK, high_part, "k", 2, 1, k_hi)
                run(MLP, gelu, "fca", 0)
                run(MLP, gelu, "fcb", 1)
                exps(t, 3)
                run(STACK, value_blocks)
                exps(t, 4)
                run(PROJ, f_by_token)
                exps(t, 5)

            steps(act, step)

        @block.vector
        def _(dve):
            nc.vector.memset(psum[:, :, :], 0.0).then_inc(psum_clear, 1)
            dve.wait_ge(consts_in, 16 * N_CONST)
            g = vec[:, G1:G1 + 1]
            nc.vector.tensor_scalar(wq[:, :], wraw[:, 0:C], g, SCALE, ALU.mult, ALU.mult)
            nc.vector.tensor_scalar(wk[:, :], wraw[:, C:2 * C], g, None, ALU.mult)
            nc.vector.tensor_scalar(wv[:, :], wraw[:, 2 * C:3 * C], g, None, ALU.mult)
            nc.vector.tensor_scalar(w1[:, :], w1raw[:, :], vec[:, G2:G2 + 1], None, ALU.mult).then_inc(weights_set, 1)
            dve.wait_ge(bias_made, 1)
            nc.vector.tensor_scalar(bias[:, 0:1], psum[0:C, 0, 0:1], vec[:, BQ:BQ + 1], SCALE, ALU.add, ALU.mult)
            for n, raw in ((1, BK), (3, BF1), (4, BF1 + 1), (2, BV)):
                last = nc.vector.tensor_tensor(bias[:, n:n + 1], psum[0:C, 0, n:n + 1], vec[:, raw:raw + 1], ALU.add)
            last.then_inc(bias_set, 1)
            dve.wait_ge(bias_made, 2)
            nc.vector.tensor_tensor(bias[:, 5:6], psum[0:C, 0, 5:6], vec[:, BP:BP + 1], ALU.add).then_inc(bias_set, 1)
            dve.wait_ge(bias_set, 2)

            def product(t, name):
                b = t.step(GENERAL[name])
                dve.wait_ge(made[name], b.count(1, 1))
                return b, psum[:, bank(t, name), :]

            def stats(b, by_token, tok, st, mv, bn, done):
                n = b.c % 2
                dve.wait_ge(by_token, b.count(1, 1))
                for p in range(PAIRS):
                    last = nc.vector.bn_stats(st[:, n, p, :], tok[:, n, p, :])
                last.then_inc(bn, 1)
                dve.wait_ge(bn, b.count(1, 1))
                alone(dve)
                for p in range(PAIRS):
                    last = nc.vector.bn_aggr(mv[:, n, p, :], st[:, n, p, :])
                last.then_inc(done, 1)

            def normalise(b, root, transposed, tok, mv, rs, xn, done):
                n = b.c % 2
                dve.wait_ge(root, b.count(1, 1))
                wait(dve, transposed, b.count(1, -1))
                for p in range(PAIRS):
                    last = nc.vector.tensor_scalar(xn[:, n, p, :], tok[:, n, p, :], mv[:, n, p, 0:1], rs[:, n, p:p + 1], ALU.subtract, ALU.mult)
                last.then_inc(done, 1)

            def maxima(t, u):
                b = t.step(SCORE)
                if has(b):
                    dve.wait_ge(s_made, b.count(UNITS, u + 1))
                    if u == 0:
                        wait(dve, made["mt"], b.count(1, -1))
                    nc.vector.tensor_reduce(nmax[:, b.c % 2, 8 * u:8 * u + 8], psum[0:PR, S_BANK + u % 2, 0:2 * CH].rearrange("i (h j) -> i h j", j=L),
                                            axis=AX.X, op=ALU.max, negate=True).then_inc(s_maxed, 1)

            def residual(t):
                b, src = product(t, "proj")
                wait(dve, f_biased, b.count(1, -3))
                wait(dve, made["nt1"], b.count(1, -3))
                nc.vector.scalar_tensor_tensor(out=f[:, b.c % 4, :], in0=src[0:C, 0:TOK], scalar=bias[:, 5:6], in1=xw[:, b.c % 8, :],
                                               op0=ALU.add, op1=ALU.add).then_inc(taken["proj"], 1)

            def low_part(t, name, part, col, high):
                b, src = product(t, name)
                n = b.c % 2
                dve.wait_ge(high, b.count(1, 1))
                nc.vector.scalar_tensor_tensor(out=nat[:, n, part + 1, :], in0=src[0:C, 0:TOK], scalar=bias[:, col:col + 1], in1=nat[:, n, part, :],
                                               op0=ALU.add, op1=ALU.subtract).then_inc(taken[name], 1)

            def block_k(b):
                dve.wait_ge(stack_in[b.c % 4], b.used(4, STACK_IN[b.c % 4]))
                wait(dve, s_made, b.count(UNITS, -UNITS))
                for h in range(4):
                    last = nc.vector.tensor_scalar(kbd[:, b.c % 2, :, h, :], kst[:, b.c % 4, :, :], heads[:, 4 + h:5 + h], None, ALU.mult)
                last.then_inc(k_blocks, 1)

            def block_q(b):
                dve.wait_ge(max_in[b.c % 2], b.used(2, QUADS * 16))
                wait(dve, p_made, b.count(UNITS, -UNITS))
                for h in range(4):
                    last = nc.vector.tensor_scalar(qbd[:, b.c % 2, :, h, :], qst[:, b.c % 4, :, :], heads[:, h:h + 1], None, ALU.mult)
                last.then_inc(q_blocks, 1)

            def divide(t, d):
                b = t.step(PROB)
                if not has(b):
                    return
                dve.wait_ge(pv_made, b.count(2, d + 1))
                src = psum[0:L, O_BANK + d, 0:2 * 2 * NH * (HD + 1)].rearrange("t (n e) -> t n e", e=HD + 1)
                nc.vector.reciprocal(rsum[:, d, :].rearrange("t (n e) -> t n e", e=1), src[:, :, HD:HD + 1]).then_inc(o_inverted, 1)
                dve.wait_ge(o_inverted, b.count(2, d + 1))
                if d == 0:
                    wait(dve, made["ot"], b.count(1, -1))
                nc.vector.tensor_tensor(on[:, b.c % 2, d * PAIRS:(d + 1) * PAIRS, :].rearrange("t n (h e) -> t (n h) e", e=HD), src[:, :, 0:HD],
                                        rsum[:, d, :].rearrange("t (n e) -> t n e", e=1).to_broadcast([L, PAIRS * NH, HD]), ALU.mult).then_inc(o_normed, 1)

            def result(t):
                b, src = product(t, "fc2")
                dve.wait_ge(f_biased, b.count(1, 1))
                wait(dve, y_out[b.c % 2], b.step(-2).used(2, 2 * 16))
                dst, res, inner = yr[:, b.c % 2, :, :], fb[:, b.c % 4, :], BANDS - 1
                parts = [(dst[:, :, SHIFT:SHIFT + inner * WS].rearrange("c r (w s) -> c w r s", s=WS),
                          *(v[:, 0:inner * L].rearrange("c (w r s) -> c w r s", w=inner, r=WS) for v in (src[0:C, :], res)))]
                ends = [v[:, inner * L:TOK].rearrange("c (r s) -> c r s", r=WS) for v in (src[0:C, :], res)]
                parts.append((dst[:, :, SIDE - WS + SHIFT:SIDE], *(v[:, :, 0:WS - SHIFT] for v in ends)))
                parts.append((dst[:, :, 0:SHIFT], *(v[:, :, WS - SHIFT:WS] for v in ends)))
                for to, a, c in parts:
                    last = nc.vector.tensor_tensor(to, a, c, ALU.add)
                last.then_inc(taken["fc2"], 1)

            def step(t):
                def run(offset, stage, *more):
                    if has(t.step(offset)):
                        stage(t, *more)

                if has(t.step(QK)):
                    normalise(t.step(QK), root1, made["t2"], tok1, mv1, rs1, xn1, normed1)
                maxima(t, 0)
                maxima(t, 1)
                if has(t.step(MLP)):
                    normalise(t.step(MLP), root2, made["nt2"], tok2, mv2, rs2, xn2, normed2)
                run(PROJ, residual)
                if has(t.step(TOKENS)):
                    stats(t.step(TOKENS), taken["t1"], tok1, st1, mv1, bn1, stats1)
                maxima(t, 2)
                run(QK, low_part, "q", 0, 0, q_hi)
                run(QK, low_part, "k", 2, 1, k_hi)
                divide(t, 0)
                maxima(t, 3)
                maxima(t, 4)
                if has(t.step(STACK)):
                    block_k(t.step(STACK))
                if has(t.step(MAXIMA)):
                    block_q(t.step(MAXIMA))
                if has(t.step(PROJ)):
                    stats(t.step(PROJ), taken["nt1"], tok2, st2, mv2, bn2, stats2)
                maxima(t, 5)
                run(MLP, result)
                divide(t, 1)

            steps(dve, step)


def constants():
    ident = np.eye(128, dtype=np.float32)
    heads = np.zeros((ROWS, 8), np.float32)
    for h in range(4):
        for part in range(3):
            heads[32 * part + HD * h:32 * part + HD * h + HD, [h, 4 + h]] = 1
        heads[MASK0:MAX0, [h, 4 + h]] = 1
        heads[MAX0 + h, h] = 1
    rows = np.zeros((2, 2, 8, QUADS, TOK), np.float16)
    for kind in range(2):
        for w in range(BANDS):
            for r in range(WS):
                for s in range(WS):
                    lower = kind == 1 and r >= WS - SHIFT
                    right = w == BANDS - 1 and s >= WS - SHIFT
                    region = 2 * lower + right
                    t = w * L + r * WS + s
                    rows[0, kind, 0:4, :, t] = -100
                    rows[0, kind, region, :, t] = 0
                    rows[1, kind, region, :, t] = 1
        rows[1, kind, 4:8] = 1
    return ident, heads, rows


_INS = ["x"] + ["L0_conv_" + n for n in ("g1", "b1", "w_qkv", "b_qkv", "w_proj", "b_proj", "g2", "b2", "w_fc1", "b_fc1", "w_fc2", "b_fc2")]


def kernel(**inputs):
    import concourse.bacc as _bacc
    from concourse.bass_utils import run_bass_kernel_spmd as _run

    nc = _bacc.Bacc("TRN2", target_bir_lowering=False, num_devices=1)
    given = {n: np.ascontiguousarray(inputs[n]) for n in _INS}
    given |= dict(zip(("ident", "heads", "rows"), constants()))
    arrays, args = {}, []
    for name, a in given.items():
        arrays[f"in_{name}_dram"] = a
        args.append(nc.dram_tensor(f"in_{name}_dram", a.shape, mybir.dt.from_np(a.dtype), kind="ExternalInput").ap())
    args.append(nc.dram_tensor("out_0_dram", given["x"].shape, F32, kind="ExternalOutput").ap())
    build(nc, *args)
    r = _run(nc, [arrays], core_ids=[0])
    return r.results[0]["out_0_dram"]
```

```python
from contextlib import ExitStack

import numpy as np
import concourse.bass as bass
import concourse.mybir as mybir

F32 = mybir.dt.float32
F16 = mybir.dt.float16
ALU = mybir.AluOpType
ACT = mybir.ActivationFunctionType
AX = mybir.AxisListType

C, SIDE, WS, SHIFT, NH = 96, 56, 7, 3, 12
HD = C // NH
L = WS * WS
BANDS = SIDE // WS
PAIRS = BANDS // 2
TOK = BANDS * L
PT = 2 * L
W1 = 64
PR = W1 + L
QUADS = NH // 4
DUOS = NH // 2
HID = 2 * C
SR = 3 * 32
MASK0, MAX0, ROWS = SR, SR + 4, SR + 8
UNITS = PAIRS * QUADS // 2
CH = 4 * L
EPS = 1e-5
SCALE = HD ** -0.5

LOAD, ORDER, TOKENS, QK, STACK, SCORE, MAXIMA, PROB, PROJ, MLP = 7, 6, 5, 4, 3, 2, 1, 0, -1, -2
GENERAL = {"t1": TOKENS, "t2": QK, "mt": MAXIMA, "ot0": PROJ, "ot1": PROJ, "nt2": MLP, "q": QK, "proj": PROJ,
           "k": QK, "fca": MLP, "fcb": MLP, "v": STACK, "nt1": PROJ, "fc2": MLP}
ORDERED = list(GENERAL)
TAKES = {name: 2 if name == "v" else 1 for name in ORDERED}
FULL = 128
FILL = 96
N_CONST = 7 + 11 + 8


class Band:

    def __init__(self, i, c):
        self.i, self.c = i, c

    def count(self, per, add=0):
        return per * self.c + add if self.i is None else self.i * (BANDS * per) + (per * self.c + add)

    def used(self, ring, per):
        fixed = (self.c // ring + 1) * per
        return fixed if self.i is None else self.i * (BANDS // ring * per) + fixed

    def image(self):
        return self.c // BANDS if self.i is None else self.i + self.c // BANDS

    def step(self, d):
        return Band(self.i, self.c + d)


def build(nc, x, g1, b1, wqkv, bqkv, wproj, bproj, g2, b2, wfc1, bfc1, wfc2, bfc2,
          ident_d, heads_d, rows_d, out):
    images = x.shape[0]
    NB = images * BANDS
    FIRST = 3 - MLP
    rounds = images - 2

    ctx = ExitStack()
    with ctx:
        def sb(name, shape, dt=F32):
            return ctx.enter_context(nc.sbuf_tensor(name, shape, dt))

        def sem(name):
            return ctx.enter_context(nc.semaphore(name))

        ident = sb("ident", [128, 128])
        heads = sb("heads", [ROWS, 10])
        wraw, w1raw = sb("wraw", [C, 3 * C]), sb("w1raw", [C, HID])
        wp = sb("wp", [C, C])
        wq, wk, wv = sb("wq", [FULL, C]), sb("wk", [FULL, C]), sb("wv", [FULL, C])
        wpd = sb("wpd", [FULL, 2, C])
        w1, w2 = sb("w1", [FULL, HID]), sb("w2", [FULL, 2, C])
        vec = sb("vec", [C, 11])
        G1, B1, BQ, BK, BV, BP, G2, B2, BF1, BF2 = 0, 1, 2, 3, 4, 5, 6, 7, 8, 10
        bias = sb("bias", [C, 6])
        half = sb("half", [128, PAIRS])
        xr = sb("xr", [C, 4, WS, SIDE])
        xw = sb("xw", [C, 8, TOK])
        tok1, tok2 = sb("tok1", [PT, 2, PAIRS, C]), sb("tok2", [PT, 2, PAIRS, C])
        st1, st2 = sb("st1", [PT, 2, PAIRS, 6]), sb("st2", [PT, 2, PAIRS, 6])
        mv1, mv2 = sb("mv1", [PT, 2, PAIRS, 2]), sb("mv2", [PT, 2, PAIRS, 2])
        ve1, ve2 = sb("ve1", [PT, 2, PAIRS]), sb("ve2", [PT, 2, PAIRS])
        rs1, rs2 = sb("rs1", [PT, 2, PAIRS]), sb("rs2", [PT, 2, PAIRS])
        xn1, xn2 = sb("xn1", [PT, 2, PAIRS, C]), sb("xn2", [PT, 2, PAIRS, C])
        xnT, fnT = sb("xnT", [FULL, 2, TOK]), sb("fnT", [FULL, 2, TOK])
        nat = sb("nat", [C, 2, 4, TOK], F16)
        qst = sb("qst", [FULL, 4, QUADS, TOK], F16)
        kst = sb("kst", [FULL, 4, QUADS, TOK], F16)
        qbd = sb("qbd", [FULL, 2, QUADS, 4, TOK], F16)
        kbd = sb("kbd", [FULL, 2, QUADS, 4, TOK], F16)
        vbd = sb("vbd", [FULL, 4, PAIRS * DUOS, 2, 2 * HD + 1])
        nmax = sb("nmax", [PR, 2, PAIRS * NH])
        mrow = sb("mrow", [PAIRS * NH, 2, PT], F16)
        probs = sb("probs", [FULL, 2, PAIRS * QUADS, CH])
        rsum = sb("rsum", [PT, 2, PAIRS * DUOS])
        on = sb("on", [PT, 2, PAIRS * 2, C])
        oT = sb("oT", [FULL, 2, BANDS, 2, L])
        f, fb = sb("f", [C, 4, TOK]), sb("fb", [C, 4, TOK])
        hid = sb("hid", [FULL, 2, 2, TOK])
        yr = sb("yr", [C, 2, WS, SIDE])

        psum = ctx.enter_context(nc.psum_tensor("psum", [128, 8, 512], F32))
        S_BANK, P_BANK, O_BANK, G_BANK = 0, 2, 4, 6

        nat_d = nc.dram_tensor("nat_d", [2, C, 4, TOK], F16, kind="Internal").ap()
        max_d = nc.dram_tensor("max_d", [2, PAIRS, NH, PT], F16, kind="Internal").ap()

        consts_in, filled, vbd_zero, vbd_ones = sem("consts_in"), sem("filled"), sem("vbd_zero"), sem("vbd_ones")
        psum_clear, weights_set = sem("psum_clear"), sem("weights_set")
        bias_made, bias_set = sem("bias_made"), sem("bias_set")
        x_in = [sem(f"x_in{n}") for n in range(4)]
        nat_out = [sem(f"nat_out{n}") for n in range(2)]
        stack_in = [sem(f"stack_in{n}") for n in range(4)]
        max_out = [sem(f"max_out{n}") for n in range(2)]
        max_in = [sem(f"max_in{n}") for n in range(2)]
        y_out = [sem(f"y_out{n}") for n in range(2)]
        STACK_IN = [6 * 16, 6 * 16, 6 * 16, 8 * 16]
        made = {name: sem(f"made_{name}") for name in ORDERED}
        taken = {name: sem(f"taken_{name}") for name in ORDERED}
        passed = sem("passed")
        x_ordered, f_biased = sem("x_ordered"), sem("f_biased")
        bn1, stats1, eps1, root1, normed1 = (sem(n) for n in ("bn1", "stats1", "eps1", "root1", "normed1"))
        bn2, stats2, eps2, root2, normed2 = (sem(n) for n in ("bn2", "stats2", "eps2", "root2", "normed2"))
        q_hi, k_hi = sem("q_hi"), sem("k_hi")
        k_blocks, q_blocks = sem("k_blocks"), sem("q_blocks")
        s_made, s_maxed = sem("s_made"), sem("s_maxed")
        p_made, exp_done = sem("p_made"), sem("exp_done")
        pv_made, o_inverted, o_normed = sem("pv_made"), sem("o_inverted"), sem("o_normed")

        block = ctx.enter_context(nc.Block())

        def steps(engine, step):
            for t in range(-LOAD, FIRST):
                step(Band(None, t))
            with engine.Fori(0, rounds) as i:
                for t in range(BANDS):
                    step(Band(i, FIRST + t))
            for t in range(FIRST + BANDS * rounds, NB - MLP):
                step(Band(None, t))

        def has(b):
            return b.i is not None or 0 <= b.c < NB

        def wait(engine, s, value):
            if not isinstance(value, int) or value > 0:
                engine.wait_ge(s, value)

        def alone(engine):
            engine.sem_inc(passed, 1)

        def bank(t, name):
            return G_BANK + (t.c * len(ORDERED) + ORDERED.index(name)) % 2

        def chunk(u, n):
            return divmod(2 * u + n, QUADS)

        def image_rows(c):
            r = (c % BANDS) * WS + SHIFT
            return [(0, r, WS - SHIFT), (WS - SHIFT, (r + WS - SHIFT) % SIDE, SHIFT)]

        @block.sync
        def _(sp):
            def const(dst, src):
                sp.dma_start(dst, src).then_inc(consts_in, 16)

            def column(n, v):
                const(vec[:, n:n + 1], v.rearrange("(c a) -> c a", a=1))

            sp.wait_ge(filled, 1)
            const(ident[:, :], ident_d)
            const(heads[:, :], heads_d)
            const(wraw[:, :], wqkv)
            const(w1raw[:, :], wfc1)
            const(wp[:, :], wproj)
            for m in range(2):
                const(w2[0:C, m, :], wfc2[m * C:(m + 1) * C, :])
                column(BF1 + m, bfc1[m * C:(m + 1) * C])
            for m in range(3):
                column(BQ + m, bqkv[m * C:(m + 1) * C])
            for n, v in ((G1, g1), (B1, b1), (BP, bproj), (G2, g2), (B2, b2), (BF2, bfc2)):
                column(n, v)
            for n in range(4):
                const(qst[MASK0:ROWS, n, :, :], rows_d[0, 0, :, :, :])
                const(kst[MASK0:ROWS, n, :, :], rows_d[1, 0, :, :, :])
            sp.wait_ge(consts_in, 16 * N_CONST)

            def load_x(b):
                n = b.c % 4
                wait(sp, x_ordered, b.count(1, -3))
                alone(sp)
                for at, row, rows in image_rows(b.c):
                    sp.dma_start(xr[:, n, at:at + rows, :], x[b.image(), :, row:row + rows, :]).then_inc(x_in[n], 16)

            def stacks(b):
                n = b.c % 4
                wait(sp, p_made, b.count(UNITS, -3 * UNITS))
                alone(sp)
                if n == 3:
                    kind = int(b.c % BANDS == BANDS - 1)
                    sp.dma_start(qst[MASK0:MAX0, n, :, :], rows_d[0, kind, 0:4, :, :]).then_inc(stack_in[n], 16)
                    sp.dma_start(kst[MASK0:MAX0, n, :, :], rows_d[1, kind, 0:4, :, :]).then_inc(stack_in[n], 16)
                sp.wait_ge(nat_out[b.c % 2], b.used(2, 16))
                alone(sp)
                src = nat_d[b.c % 2, :, :, :].rearrange("(c r) n t -> n r c t", c=QUADS)
                for stack, parts in ((kst, (2, 3, 2)), (qst, (0, 0, 1))):
                    for m, part in enumerate(parts):
                        sp.dma_start(stack[32 * m:32 * m + 32, n, :, :], src[part, :, :, :]).then_inc(stack_in[n], 16)

            def maxima(b):
                n = b.c % 2
                wait(sp, max_in[n], b.step(-2).used(2, QUADS * 16))
                alone(sp)
                sp.wait_ge(taken["mt"], b.count(1, 1))
                alone(sp)
                sp.dma_start(max_d[n, :, :, :].rearrange("p h t -> (p h) t"), mrow[:, n, :]).then_inc(max_out[n], 16)
                sp.wait_ge(max_out[n], b.used(2, 16))
                alone(sp)
                for c in range(QUADS):
                    sp.dma_start(qst[MAX0:ROWS, b.c % 4, c, :].rearrange("h (p t) -> h p t", t=PT),
                                 max_d[n, :, 4 * c:4 * c + 4, :].rearrange("p h t -> h p t")).then_inc(max_in[n], 16)

            def save_parts(b):
                n = b.c % 2
                wait(sp, stack_in[(b.c - 2) % 4], b.step(-2).used(4, STACK_IN[(b.c - 2) % 4]))
                alone(sp)
                sp.wait_ge(taken["q"], b.count(1, 1))
                alone(sp)
                sp.wait_ge(taken["k"], b.count(1, 1))
                alone(sp)
                sp.dma_start(nat_d[n, :, :, :], nat[:, n, :, :]).then_inc(nat_out[n], 16)

            def store_y(b):
                n = b.c % 2
                sp.wait_ge(taken["fc2"], b.count(1, 1))
                alone(sp)
                for at, row, rows in image_rows(b.c):
                    sp.dma_start(out[b.image(), :, row:row + rows, :], yr[:, n, at:at + rows, :]).then_inc(y_out[n], 16)

            def step(t):
                for offset, stage in ((LOAD, load_x), (STACK, stacks), (MAXIMA, maxima), (QK, save_parts), (MLP, store_y)):
                    if has(t.step(offset)):
                        stage(t.step(offset))

            steps(sp, step)
            for n in range(2):
                sp.wait_ge(y_out[n], 2 * 16 * NB // 2)

        @block.gpsimd
        def _(pool):
            nc.gpsimd.memset(half[:, :], -0.5)
            nc.gpsimd.memset(vbd[:, :, :, :, :], 0.0).then_inc(vbd_zero, 1)
            pool.wait_ge(vbd_zero, 1)
            nc.gpsimd.memset(vbd[0:L, :, :, 0, 2 * HD:2 * HD + 1], 1.0)
            nc.gpsimd.memset(vbd[W1:PR, :, :, 1, 2 * HD:2 * HD + 1], 1.0).then_inc(vbd_ones, 1)
            pool.wait_ge(vbd_ones, 1)
            pool.wait_ge(consts_in, 16 * N_CONST)

            def order_x(b):
                pool.wait_ge(x_in[b.c % 4], b.used(4, 2 * 16))
                alone(pool)
                wait(pool, taken["proj"], b.count(1, -7))
                alone(pool)
                src, dst, inner = xr[:, b.c % 4, :, :], xw[:, b.c % 8, :], BANDS - 1
                nc.gpsimd.tensor_copy(dst[:, 0:inner * L].rearrange("c (w r s) -> c w r s", w=inner, r=WS),
                                      src[:, :, SHIFT:SHIFT + inner * WS].rearrange("c r (w s) -> c w r s", s=WS))
                end = dst[:, inner * L:TOK].rearrange("c (r s) -> c r s", r=WS)
                nc.gpsimd.tensor_copy(end[:, :, 0:WS - SHIFT], src[:, :, SIDE - WS + SHIFT:SIDE])
                nc.gpsimd.tensor_copy(end[:, :, WS - SHIFT:WS], src[:, :, 0:SHIFT]).then_inc(x_ordered, 1)

            def add_bias(b):
                n = b.c % 4
                pool.wait_ge(taken["proj"], b.count(1, 1))
                alone(pool)
                wait(pool, taken["fc2"], b.count(1, -3))
                alone(pool)
                nc.gpsimd.tensor_scalar(fb[:, n, :], f[:, n, :], vec[:, BF2:BF2 + 1], None, ALU.add).then_inc(f_biased, 1)

            def root(b, mv, ve, rs, stats, eps, done):
                n = b.c % 2
                pool.wait_ge(stats, b.count(1, 1))
                alone(pool)
                nc.gpsimd.tensor_scalar(ve[:, n, :], mv[:, n, :, 1], EPS, None, ALU.add).then_inc(eps, 1)
                pool.wait_ge(eps, b.count(1, 1))
                alone(pool)
                nc.gpsimd.tensor_tensor(rs[:, n, :], ve[:, n, :], half[0:PT, :], ALU.pow).then_inc(done, 1)

            def step(t):
                if has(t.step(ORDER)):
                    order_x(t.step(ORDER))
                if has(t.step(TOKENS)):
                    root(t.step(TOKENS), mv1, ve1, rs1, stats1, eps1, root1)
                if has(t.step(PROJ)):
                    add_bias(t.step(PROJ))
                if has(t.step(PROJ)):
                    root(t.step(PROJ), mv2, ve2, rs2, stats2, eps2, root2)

            steps(pool, step)

        @block.tensor
        def _(pe):
            pe.wait_ge(consts_in, 16 * N_CONST)
            pe.wait_ge(psum_clear, 1)
            for n in range(3):
                nc.tensor.matmul(psum[0:C, 0, n:n + 1], wraw[:, n * C:(n + 1) * C], vec[:, B1:B1 + 1], start=True, stop=True)
            for n in range(2):
                last = nc.tensor.matmul(psum[0:C, 0, 3 + n:4 + n], w1raw[:, n * C:(n + 1) * C], vec[:, B2:B2 + 1], start=True, stop=True)
            last.then_inc(bias_made, 1)
            pe.wait_ge(bias_set, 1)
            nc.tensor.matmul(psum[0:C, 0, 5:6], wp[:, :], bias[:, 2:3], start=True, stop=True).then_inc(bias_made, 1)
            pe.wait_ge(bias_set, 2)
            pe.wait_ge(weights_set, 1)
            pe.wait_ge(vbd_ones, 1)

            def general(t, name):
                at = t.c * len(ORDERED) + ORDERED.index(name) - 2
                while True:
                    c, n = divmod(at, len(ORDERED))
                    before = Band(t.i, c + GENERAL[ORDERED[n]])
                    if has(before):
                        per = TAKES[ORDERED[n]]
                        pe.wait_ge(taken[ORDERED[n]], before.count(per, per))
                        break
                    at -= 2
                    if at < -LOAD * len(ORDERED):
                        break
                return psum[:, bank(t, name), :]

            def transposes(t, name, ready, src, rows):
                b = t.step(GENERAL[name])
                if not has(b):
                    return
                pe.wait_ge(ready, b.count(1, 1))
                dst = general(t, name)
                for p in range(PAIRS):
                    part = src(b, p)
                    other = PT + C - rows
                    last = nc.tensor.transpose(dst[0:other, p * rows:(p + 1) * rows], part, ident[0:rows, 0:rows])
                last.then_inc(made[name], 1)

            def dense(t, name, ready, parts):
                b = t.step(GENERAL[name])
                if not has(b):
                    return
                pe.wait_ge(ready, b.count(1, 1))
                dst = general(t, name)
                parts = parts(b)
                for n, (weights, tokens) in enumerate(parts):
                    last = nc.tensor.matmul(dst[0:C, 0:TOK], weights, tokens, start=n == 0, stop=n == len(parts) - 1)
                last.then_inc(made[name], 1)

            def values(t):
                b = t.step(STACK)
                if not has(b):
                    return
                dst = general(t, "v")
                for p in range(PAIRS):
                    for w in range(2):
                        at = (2 * p + w) * L
                        last = nc.tensor.matmul(dst[W1 * w:W1 * w + L, p * C:(p + 1) * C], xnT[:, b.c % 2, at:at + L], wv[:, :], start=True, stop=True)
                last.then_inc(made["v"], 1)

            def out_transposes(t, d):
                b = t.step(PROJ)
                if not has(b):
                    return
                pe.wait_ge(o_normed, b.count(2, d + 1))
                dst = general(t, f"ot{d}")
                for n in range(PAIRS):
                    last = nc.tensor.transpose(dst[0:C, n * PT:(n + 1) * PT], on[:, b.c % 2, d * PAIRS + n, :], ident[0:PT, 0:PT])
                last.then_inc(made[f"ot{d}"], 1)

            def max_transpose(t):
                b = t.step(MAXIMA)
                if not has(b):
                    return
                pe.wait_ge(s_maxed, b.count(UNITS, UNITS))
                dst = general(t, "mt")
                alone(pe)
                nc.tensor.transpose(dst[0:PAIRS * NH, 0:PR], nmax[:, b.c % 2, :], ident[0:PR, 0:PR]).then_inc(made["mt"], 1)

            def score_bank(b, u, first_bank, side, blocks, done):
                for n in range(2):
                    p, c = chunk(u, n)
                    for w in range(2):
                        at = (2 * p + w) * L
                        last = nc.tensor.matmul(psum[W1 * w:W1 * w + L, first_bank + u % 2, n * CH:(n + 1) * CH],
                                                side[:, b.c % 4, c, at:at + L], blocks[:, b.c % 2, c, :, at:at + L], start=True, stop=True)
                last.then_inc(done, 1)

            def scores(t, u):
                b = t.step(SCORE)
                if has(b):
                    if u == 0:
                        pe.wait_ge(k_blocks, b.count(1, 1))
                    wait(pe, s_maxed, b.count(UNITS, u - 1))
                    score_bank(b, u, S_BANK, qst, kbd, s_made)

            def shifted(t, u):
                b = t.step(PROB)
                if has(b):
                    if u == 0:
                        pe.wait_ge(q_blocks, b.count(1, 1))
                    wait(pe, exp_done, b.count(UNITS, u - 1))
                    score_bank(b, u, P_BANK, kst, qbd, p_made)

            def weighted(t, p):
                b = t.step(PROB if p < PAIRS - 1 else PROJ)
                if not has(b):
                    return
                if p == 0:
                    pe.wait_ge(taken["v"], b.count(2, 2))
                pe.wait_ge(exp_done, b.count(UNITS, (QUADS * p + QUADS - 1) // 2 + 1))
                if p % 2 == 0:
                    wait(pe, o_normed, b.count(2, p // 2 - 1))
                dst = psum[0:PT, O_BANK + p // 2, 0:2 * 2 * DUOS * (2 * HD + 1)].rearrange("t (p w h e) -> t p w h e", p=2, w=2, h=DUOS)
                for h in range(DUOS):
                    last = nc.tensor.matmul(dst[:, p % 2, :, h, :],
                                            probs[:, b.c % 2, p * QUADS + h // 2, h % 2 * PT:(h % 2 + 1) * PT],
                                            vbd[:, b.c % 4, p * DUOS + h, :, :], start=True, stop=True)
                if p % 2:
                    last.then_inc(pv_made, 1)

            def step(t):
                shifted(t, 0)
                scores(t, 0)
                weighted(t, 3)
                transposes(t, "t1", x_ordered, lambda b, p: xw[:, b.c % 8, p * PT:(p + 1) * PT], C)
                shifted(t, 1)
                scores(t, 1)
                transposes(t, "t2", normed1, lambda b, p: xn1[:, b.c % 2, p, :], PT)
                max_transpose(t)
                shifted(t, 2)
                scores(t, 2)
                out_transposes(t, 0)
                out_transposes(t, 1)
                transposes(t, "nt2", normed2, lambda b, p: xn2[:, b.c % 2, p, :], PT)
                shifted(t, 3)
                scores(t, 3)
                weighted(t, 0)
                dense(t, "q", taken["t2"], lambda b: [(wq[:, :], xnT[:, b.c % 2, :])])
                dense(t, "proj", taken["ot1"], lambda b: [(wpd[:, m, :], oT[:, b.c % 2, :, m, :]) for m in range(2)])
                shifted(t, 4)
                scores(t, 4)
                dense(t, "k", taken["t2"], lambda b: [(wk[:, :], xnT[:, b.c % 2, :])])
                weighted(t, 1)
                dense(t, "fca", taken["nt2"], lambda b: [(w1[:, 0:C], fnT[:, b.c % 2, :])])
                dense(t, "fcb", taken["nt2"], lambda b: [(w1[:, C:HID], fnT[:, b.c % 2, :])])
                shifted(t, 5)
                scores(t, 5)
                values(t)
                weighted(t, 2)
                transposes(t, "nt1", taken["proj"], lambda b, p: f[:, b.c % 4, p * PT:(p + 1) * PT], C)
                dense(t, "fc2", taken["fcb"], lambda b: [(w2[:, m, :], hid[:, b.c % 2, m, :]) for m in range(2)])

            steps(pe, step)

        @block.scalar
        def _(act):
            act.wait_ge(bias_set, 2)
            act.wait_ge(vbd_ones, 1)

            def product(t, name):
                b = t.step(GENERAL[name])
                act.wait_ge(made[name], b.count(1, 1))
                return b, psum[:, bank(t, name), :]

            def out_by_channel(t, d):
                b, src = product(t, f"ot{d}")
                if d == 0:
                    wait(act, made["proj"], b.count(1, -1))
                nc.scalar.activation(oT[0:C, b.c % 2, d * PAIRS:(d + 1) * PAIRS, :, :],
                                     src[0:C, 0:PAIRS * PT].rearrange("c (n h t) -> c n h t", n=PAIRS, h=2), ACT.Copy).then_inc(taken[f"ot{d}"], 1)

            def max_rows(t):
                b, src = product(t, "mt")
                wait(act, max_out[b.c % 2], b.step(-2).used(2, 16))
                nc.scalar.activation(mrow[:, b.c % 2, :].rearrange("h (w t) -> h w t", w=2),
                                     src[0:PAIRS * NH, 0:2 * W1].rearrange("h (w t) -> h w t", w=2)[:, :, 0:L],
                                     ACT.Copy).then_inc(taken["mt"], 1)

            def x_by_channel(t):
                b, src = product(t, "t2")
                wait(act, made["v"], b.count(1, -1))
                nc.scalar.activation(xnT[0:C, b.c % 2, :], src[0:C, 0:TOK], ACT.Copy).then_inc(taken["t2"], 1)

            def x_by_token(t):
                b, src = product(t, "t1")
                wait(act, normed1, b.count(1, -1))
                nc.scalar.activation(tok1[:, b.c % 2, :, :], src[0:PT, 0:PAIRS * C].rearrange("t (p c) -> t p c", c=C), ACT.Copy).then_inc(taken["t1"], 1)

            def f_by_channel(t):
                b, src = product(t, "nt2")
                wait(act, made["fcb"], b.count(1, -1))
                nc.scalar.activation(fnT[0:C, b.c % 2, :], src[0:C, 0:TOK], ACT.Copy).then_inc(taken["nt2"], 1)

            def f_by_token(t):
                b, src = product(t, "nt1")
                wait(act, normed2, b.count(1, -1))
                nc.scalar.activation(tok2[:, b.c % 2, :, :], src[0:PT, 0:PAIRS * C].rearrange("t (p c) -> t p c", c=C), ACT.Copy).then_inc(taken["nt1"], 1)

            def high_part(t, name, part, col, done):
                b, src = product(t, name)
                if name == "q":
                    wait(act, nat_out[b.c % 2], b.step(-2).used(2, 16))
                nc.scalar.activation(nat[:, b.c % 2, part, :], src[0:C, 0:TOK], ACT.Identity, bias=bias[:, col:col + 1]).then_inc(done, 1)

            def value_blocks(t):
                b, src = product(t, "v")
                wait(act, pv_made, b.count(2, -6))
                for w in range(2):
                    rows = slice(W1 * w, W1 * w + L)
                    nc.scalar.activation(vbd[rows, b.c % 4, :, w, 0:2 * HD], src[rows, 0:PAIRS * C].rearrange("t (h d) -> t h d", d=2 * HD),
                                         ACT.Copy).then_inc(taken["v"], 1)

            def exps(t, u):
                b = t.step(PROB)
                if has(b):
                    act.wait_ge(p_made, b.count(UNITS, u + 1))
                    if u == 0:
                        wait(act, pv_made, b.count(2, -2))
                    nc.scalar.activation(probs[0:PR, b.c % 2, 2 * u:2 * u + 2, :], psum[0:PR, P_BANK + u % 2, 0:2 * CH].rearrange("j (n k) -> j n k", n=2),
                                         ACT.Exp).then_inc(exp_done, 1)

            def gelu(t, name, m):
                b, src = product(t, name)
                if m == 0:
                    wait(act, made["fc2"], b.count(1, -1))
                nc.scalar.activation(hid[0:C, b.c % 2, m, :], src[0:C, 0:TOK], ACT.Gelu, bias=bias[:, 3 + m:4 + m]).then_inc(taken[name], 1)

            def step(t):
                def run(offset, stage, *more):
                    if has(t.step(offset)):
                        stage(t, *more)

                exps(t, 0)
                run(TOKENS, x_by_token)
                exps(t, 1)
                run(QK, x_by_channel)
                run(MAXIMA, max_rows)
                exps(t, 2)
                run(PROJ, out_by_channel, 0)
                run(PROJ, out_by_channel, 1)
                run(MLP, f_by_channel)
                exps(t, 3)
                run(QK, high_part, "q", 0, 0, q_hi)
                exps(t, 4)
                run(QK, high_part, "k", 2, 1, k_hi)
                run(MLP, gelu, "fca", 0)
                run(MLP, gelu, "fcb", 1)
                exps(t, 5)
                run(STACK, value_blocks)
                run(PROJ, f_by_token)

            steps(act, step)

        @block.vector
        def _(dve):
            for a in (wq, wk, wv, wpd, w1, w2, xnT, fnT, oT, hid, qst, kst, qbd, kbd, probs):
                last = nc.vector.memset(a[FILL:FULL], 0.0)
            last.then_inc(filled, 1)
            dve.wait_ge(filled, 1)
            nc.vector.memset(psum[:, :, :], 0.0).then_inc(psum_clear, 1)
            dve.wait_ge(consts_in, 16 * N_CONST)
            g = vec[:, G1:G1 + 1]
            nc.vector.tensor_scalar(wq[0:C, :], wraw[:, 0:C], g, SCALE, ALU.mult, ALU.mult)
            nc.vector.tensor_scalar(wk[0:C, :], wraw[:, C:2 * C], g, None, ALU.mult)
            nc.vector.tensor_scalar(wv[0:C, :], wraw[:, 2 * C:3 * C], g, None, ALU.mult)
            nc.vector.tensor_scalar(w1[0:C, :], w1raw[:, :], vec[:, G2:G2 + 1], None, ALU.mult).then_inc(weights_set, 1)
            for m in range(2):
                nc.vector.tensor_scalar(wpd[0:C, m, :], wp[:, :], heads[0:C, 8 + m:9 + m], None, ALU.mult)
            dve.wait_ge(bias_made, 1)
            nc.vector.tensor_scalar(bias[:, 0:1], psum[0:C, 0, 0:1], vec[:, BQ:BQ + 1], SCALE, ALU.add, ALU.mult)
            for n, raw in ((1, BK), (3, BF1), (4, BF1 + 1), (2, BV)):
                last = nc.vector.tensor_tensor(bias[:, n:n + 1], psum[0:C, 0, n:n + 1], vec[:, raw:raw + 1], ALU.add)
            last.then_inc(bias_set, 1)
            dve.wait_ge(bias_made, 2)
            nc.vector.tensor_tensor(bias[:, 5:6], psum[0:C, 0, 5:6], vec[:, BP:BP + 1], ALU.add).then_inc(bias_set, 1)
            dve.wait_ge(bias_set, 2)

            def product(t, name):
                b = t.step(GENERAL[name])
                dve.wait_ge(made[name], b.count(1, 1))
                return b, psum[:, bank(t, name), :]

            def stats(b, by_token, tok, st, mv, bn, done):
                n = b.c % 2
                dve.wait_ge(by_token, b.count(1, 1))
                for p in range(PAIRS):
                    last = nc.vector.bn_stats(st[:, n, p, :], tok[:, n, p, :])
                last.then_inc(bn, 1)
                dve.wait_ge(bn, b.count(1, 1))
                alone(dve)
                for p in range(PAIRS):
                    last = nc.vector.bn_aggr(mv[:, n, p, :], st[:, n, p, :])
                last.then_inc(done, 1)

            def normalise(b, root, transposed, tok, mv, rs, xn, done):
                n = b.c % 2
                dve.wait_ge(root, b.count(1, 1))
                wait(dve, transposed, b.count(1, -1))
                for p in range(PAIRS):
                    last = nc.vector.tensor_scalar(xn[:, n, p, :], tok[:, n, p, :], mv[:, n, p, 0:1], rs[:, n, p:p + 1], ALU.subtract, ALU.mult)
                last.then_inc(done, 1)

            def maxima(t, u):
                b = t.step(SCORE)
                if has(b):
                    dve.wait_ge(s_made, b.count(UNITS, u + 1))
                    if u == 0:
                        wait(dve, made["mt"], b.count(1, -1))
                    nc.vector.tensor_reduce(nmax[:, b.c % 2, 8 * u:8 * u + 8], psum[0:PR, S_BANK + u % 2, 0:2 * CH].rearrange("i (h j) -> i h j", j=L),
                                            axis=AX.X, op=ALU.max, negate=True).then_inc(s_maxed, 1)

            def residual(t):
                b, src = product(t, "proj")
                wait(dve, f_biased, b.count(1, -3))
                wait(dve, made["nt1"], b.count(1, -3))
                nc.vector.scalar_tensor_tensor(out=f[:, b.c % 4, :], in0=src[0:C, 0:TOK], scalar=bias[:, 5:6], in1=xw[:, b.c % 8, :],
                                               op0=ALU.add, op1=ALU.add).then_inc(taken["proj"], 1)

            def low_part(t, name, part, col, high):
                b, src = product(t, name)
                n = b.c % 2
                dve.wait_ge(high, b.count(1, 1))
                nc.vector.scalar_tensor_tensor(out=nat[:, n, part + 1, :], in0=src[0:C, 0:TOK], scalar=bias[:, col:col + 1], in1=nat[:, n, part, :],
                                               op0=ALU.add, op1=ALU.subtract).then_inc(taken[name], 1)

            def block_k(t, heads_now):
                b = t.step(STACK)
                if not has(b):
                    return
                if 0 in heads_now:
                    dve.wait_ge(stack_in[b.c % 4], b.used(4, STACK_IN[b.c % 4]))
                    wait(dve, s_made, b.count(UNITS, -UNITS))
                for h in heads_now:
                    last = nc.vector.tensor_scalar(kbd[0:ROWS, b.c % 2, :, h, :], kst[0:ROWS, b.c % 4, :, :], heads[:, 4 + h:5 + h], None, ALU.mult)
                if 3 in heads_now:
                    last.then_inc(k_blocks, 1)

            def block_q(t, heads_now):
                b = t.step(MAXIMA)
                if not has(b):
                    return
                if 0 in heads_now:
                    dve.wait_ge(max_in[b.c % 2], b.used(2, QUADS * 16))
                    wait(dve, p_made, b.count(UNITS, -UNITS))
                for h in heads_now:
                    last = nc.vector.tensor_scalar(qbd[0:ROWS, b.c % 2, :, h, :], qst[0:ROWS, b.c % 4, :, :], heads[:, h:h + 1], None, ALU.mult)
                if 3 in heads_now:
                    last.then_inc(q_blocks, 1)

            def divide(t, d):
                b = t.step(PROB if d == 0 else PROJ)
                if not has(b):
                    return
                dve.wait_ge(pv_made, b.count(2, d + 1))
                src = psum[0:PT, O_BANK + d, 0:2 * 2 * DUOS * (2 * HD + 1)].rearrange("t (n e) -> t n e", e=2 * HD + 1)
                nc.vector.reciprocal(rsum[:, d, :].rearrange("t (n e) -> t n e", e=1), src[:, :, 2 * HD:2 * HD + 1]).then_inc(o_inverted, 1)
                dve.wait_ge(o_inverted, b.count(2, d + 1))
                if d == 0:
                    wait(dve, made["ot1"], b.count(1, -1))
                nc.vector.tensor_tensor(on[:, b.c % 2, d * PAIRS:(d + 1) * PAIRS, :].rearrange("t n (h e) -> t (n h) e", e=2 * HD), src[:, :, 0:2 * HD],
                                        rsum[:, d, :].rearrange("t (n e) -> t n e", e=1).to_broadcast([PT, PAIRS * DUOS, 2 * HD]), ALU.mult).then_inc(o_normed, 1)

            def result(t):
                b, src = product(t, "fc2")
                dve.wait_ge(f_biased, b.count(1, 1))
                wait(dve, y_out[b.c % 2], b.step(-2).used(2, 2 * 16))
                dst, res, inner = yr[:, b.c % 2, :, :], fb[:, b.c % 4, :], BANDS - 1
                parts = [(dst[:, :, SHIFT:SHIFT + inner * WS].rearrange("c r (w s) -> c w r s", s=WS),
                          *(v[:, 0:inner * L].rearrange("c (w r s) -> c w r s", w=inner, r=WS) for v in (src[0:C, :], res)))]
                ends = [v[:, inner * L:TOK].rearrange("c (r s) -> c r s", r=WS) for v in (src[0:C, :], res)]
                parts.append((dst[:, :, SIDE - WS + SHIFT:SIDE], *(v[:, :, 0:WS - SHIFT] for v in ends)))
                parts.append((dst[:, :, 0:SHIFT], *(v[:, :, WS - SHIFT:WS] for v in ends)))
                for to, a, c in parts:
                    last = nc.vector.tensor_tensor(to, a, c, ALU.add)
                last.then_inc(taken["fc2"], 1)

            def step(t):
                def run(offset, stage, *more):
                    if has(t.step(offset)):
                        stage(t, *more)

                maxima(t, 0)
                if has(t.step(QK)):
                    normalise(t.step(QK), root1, made["t2"], tok1, mv1, rs1, xn1, normed1)
                divide(t, 1)
                maxima(t, 1)
                if has(t.step(MLP)):
                    normalise(t.step(MLP), root2, made["nt2"], tok2, mv2, rs2, xn2, normed2)
                if has(t.step(TOKENS)):
                    stats(t.step(TOKENS), taken["t1"], tok1, st1, mv1, bn1, stats1)
                maxima(t, 2)
                block_k(t, (0, 1))
                maxima(t, 3)
                run(QK, low_part, "q", 0, 0, q_hi)
                run(PROJ, residual)
                block_k(t, (2, 3))
                maxima(t, 4)
                run(QK, low_part, "k", 2, 1, k_hi)
                block_q(t, (0, 1))
                divide(t, 0)
                maxima(t, 5)
                block_q(t, (2, 3))
                if has(t.step(PROJ)):
                    stats(t.step(PROJ), taken["nt1"], tok2, st2, mv2, bn2, stats2)
                run(MLP, result)

            steps(dve, step)


def constants():
    ident = np.eye(128, dtype=np.float32)
    heads = np.zeros((ROWS, 10), np.float32)
    for h in range(NH):
        heads[HD * h:HD * (h + 1), 8 + h % 2] = 1
    for h in range(4):
        for part in range(3):
            heads[32 * part + HD * h:32 * part + HD * h + HD, [h, 4 + h]] = 1
        heads[MASK0:MAX0, [h, 4 + h]] = 1
        heads[MAX0 + h, h] = 1
    rows = np.zeros((2, 2, 8, QUADS, TOK), np.float16)
    for kind in range(2):
        for w in range(BANDS):
            for r in range(WS):
                for s in range(WS):
                    lower = kind == 1 and r >= WS - SHIFT
                    right = w == BANDS - 1 and s >= WS - SHIFT
                    region = 2 * lower + right
                    t = w * L + r * WS + s
                    rows[0, kind, 0:4, :, t] = -100
                    rows[0, kind, region, :, t] = 0
                    rows[1, kind, region, :, t] = 1
        rows[1, kind, 4:8] = 1
    return ident, heads, rows


_INS = ["x"] + ["L0_conv_" + n for n in ("g1", "b1", "w_qkv", "b_qkv", "w_proj", "b_proj", "g2", "b2", "w_fc1", "b_fc1", "w_fc2", "b_fc2")]


def kernel(**inputs):
    import concourse.bacc as _bacc
    from concourse.bass_utils import run_bass_kernel_spmd as _run

    nc = _bacc.Bacc("TRN2", target_bir_lowering=False, num_devices=1)
    given = {n: np.ascontiguousarray(inputs[n]) for n in _INS}
    given |= dict(zip(("ident", "heads", "rows"), constants()))
    arrays, args = {}, []
    for name, a in given.items():
        arrays[f"in_{name}_dram"] = a
        args.append(nc.dram_tensor(f"in_{name}_dram", a.shape, mybir.dt.from_np(a.dtype), kind="ExternalInput").ap())
    args.append(nc.dram_tensor("out_0_dram", given["x"].shape, F32, kind="ExternalOutput").ap())
    build(nc, *args)
    r = _run(nc, [arrays], core_ids=[0])
    return r.results[0]["out_0_dram"]
```

```python
from contextlib import ExitStack

import numpy as np
import concourse.bass as bass
import concourse.mybir as mybir

F32 = mybir.dt.float32
F16 = mybir.dt.float16
ALU = mybir.AluOpType
ACT = mybir.ActivationFunctionType
AX = mybir.AxisListType

C, SIDE, WS, SHIFT, NH = 96, 56, 7, 3, 12
HD = C // NH
L = WS * WS
BANDS = SIDE // WS
PAIRS = BANDS // 2
TOK = BANDS * L
PT = 2 * L
W1 = 64
PR = W1 + L
QUADS = NH // 4
HID = 2 * C
SR = 3 * 32
MASK0, MAX0, ROWS = SR, SR + 4, SR + 8
UNITS = PAIRS * QUADS // 2
CH = 4 * L
EPS = 1e-5
SCALE = HD ** -0.5

LOAD, ORDER, TOKENS, QK, KBLOCK, STACK, SCORE, MAXIMA, QBLOCK, PROB, PROJ, NORM2 = 8, 7, 6, 5, 4, 3, 3, 2, 1, 0, -1, -2
HIDDEN, RESULT = (-3, -2), (-4, -3)
GENERAL = {"t2": QK, "t1": TOKENS, "mt": MAXIMA, "q": QK, "ot": PROJ, "nt2": NORM2, "k": QK,
           "proj": PROJ, "fca0": HIDDEN[0], "fcb0": HIDDEN[0], "fca1": HIDDEN[1], "fc20": RESULT[0],
           "fcb1": HIDDEN[1], "nt1": PROJ, "v": STACK, "fc21": RESULT[1]}
ORDERED = list(GENERAL)
PAIRED = {name: name[:3] != "fc2" for name in ORDERED if name[:2] == "fc"}
G_BANKS = 3
TAKES = {name: 2 if name in ("v", "ot") else 1 for name in ORDERED}
FULL = 128
FILL = 96


def ring(names):
    return {name: n % G_BANKS if n < len(names) - 1 or n % G_BANKS else 1 for n, name in enumerate(names)}


BANK = [ring([name for name in ORDERED if PAIRED.get(name, odd) == odd]) for odd in range(2)]
N_CONST = 7 + 11 + 1 + 8


class Band:

    def __init__(self, i, c):
        self.i, self.c = i, c

    def count(self, per, add=0):
        return per * self.c + add if self.i is None else self.i * (BANDS * per) + (per * self.c + add)

    def used(self, ring, per):
        fixed = (self.c // ring + 1) * per
        return fixed if self.i is None else self.i * (BANDS // ring * per) + fixed

    def image(self):
        return self.c // BANDS if self.i is None else self.i + self.c // BANDS

    def step(self, d):
        return Band(self.i, self.c + d)


def build(nc, x, g1, b1, wqkv, bqkv, wproj, bproj, g2, b2, wfc1, bfc1, wfc2, bfc2,
          ident_d, heads_d, rows_d, out):
    images = x.shape[0]
    NB = images * BANDS
    FIRST = 3 - NORM2
    rounds = images - 2

    ctx = ExitStack()
    with ctx:
        def sb(name, shape, dt=F32):
            return ctx.enter_context(nc.sbuf_tensor(name, shape, dt))

        def sem(name):
            return ctx.enter_context(nc.semaphore(name))

        ident = sb("ident", [128, 128])
        heads = sb("heads", [ROWS, 7])
        wraw, w1raw = sb("wraw", [C, 3 * C]), sb("w1raw", [C, HID])
        wq, wk, wv, wp = sb("wq", [FULL, C]), sb("wk", [FULL, C]), sb("wv", [FULL, C]), sb("wp", [FULL, C])
        w1, w2 = sb("w1", [FULL, HID]), sb("w2", [FULL, 2, C])
        vec = sb("vec", [C, 10])
        G1, B1, BQ, BK, BV, BP, G2, B2, BF1 = 0, 1, 2, 3, 4, 5, 6, 7, 8
        bias = sb("bias", [C, 6])
        regions = sb("regions", [4, 2, 2, TOK], F16)
        half = sb("half", [128, PAIRS])
        xr = sb("xr", [C, 4, WS, SIDE])
        xw = sb("xw", [C, 8, TOK])
        tok1, tok2 = sb("tok1", [PT, 2, PAIRS, C]), sb("tok2", [PT, 2, PAIRS, C])
        st1, st2 = sb("st1", [PT, 2, PAIRS, 6]), sb("st2", [PT, 2, PAIRS, 6])
        mv1, mv2 = sb("mv1", [PT, 2, PAIRS, 2]), sb("mv2", [PT, 2, PAIRS, 2])
        ve1, ve2 = sb("ve1", [PT, 2, PAIRS]), sb("ve2", [PT, 2, PAIRS])
        rs1, rs2 = sb("rs1", [PT, 2, PAIRS]), sb("rs2", [PT, 2, PAIRS])
        xn1, xn2 = sb("xn1", [PT, 2, PAIRS, C]), sb("xn2", [PT, 2, PAIRS, C])
        xnT, fnT = sb("xnT", [FULL, 4, TOK]), sb("fnT", [FULL, 2, TOK])
        nat = sb("nat", [C, 4, 4, TOK], F16)
        qst = sb("qst", [FULL, 4, QUADS, TOK], F16)
        kst = sb("kst", [FULL, 4, QUADS, TOK], F16)
        qbd = sb("qbd", [FULL, 2, QUADS, 4, TOK], F16)
        kbd = sb("kbd", [FULL, 2, 4, TOK], F16)
        qsd = sb("qsd", [FULL, 2, QUADS, TOK], F16)
        vbd = sb("vbd", [FULL, 4, PAIRS * NH, 2, HD + 1])
        nmax = sb("nmax", [PR, 2, PAIRS * NH])
        mrow = sb("mrow", [PAIRS * NH, 2, PT], F16)
        probs = sb("probs", [FULL, 2, PAIRS * QUADS, CH])
        rsum = sb("rsum", [PR, 2, 2 * NH])
        on = sb("on", [PR, 2, 2, 2, C])
        oT = sb("oT", [FULL, 2, TOK])
        f = sb("f", [C, 4, TOK])
        hid = sb("hid", [FULL, 2, 2, TOK])
        yr = sb("yr", [C, 2, WS, SIDE])

        psum = ctx.enter_context(nc.psum_tensor("psum", [128, 8, 512], F32))
        S_BANK, P_BANK, O_BANK, G_BANK, O_HALF = 0, 2, 4, 5, 256

        nat_d = nc.dram_tensor("nat_d", [4, C, 4, TOK], F16, kind="Internal").ap()
        max_d = nc.dram_tensor("max_d", [2, PAIRS, NH, PT], F16, kind="Internal").ap()

        consts_in, filled, hid_one, vbd_zero, vbd_ones = sem("consts_in"), sem("filled"), sem("hid_one"), sem("vbd_zero"), sem("vbd_ones")
        psum_clear, weights_set = sem("psum_clear"), sem("weights_set")
        bias_made, bias_set = sem("bias_made"), sem("bias_set")
        x_in = [sem(f"x_in{n}") for n in range(4)]
        nat_out = [sem(f"nat_out{n}") for n in range(4)]
        stack_in = [sem(f"stack_in{n}") for n in range(4)]
        max_out = [sem(f"max_out{n}") for n in range(2)]
        max_in = [sem(f"max_in{n}") for n in range(2)]
        y_out = [sem(f"y_out{n}") for n in range(2)]
        STACK_IN = [6 * 16, 6 * 16, 6 * 16, 8 * 16]
        made = {name: sem(f"made_{name}") for name in ORDERED}
        taken = {name: sem(f"taken_{name}") for name in ORDERED}
        passed = sem("passed")
        x_ordered = sem("x_ordered")
        bn1, stats1, eps1, root1, normed1 = (sem(n) for n in ("bn1", "stats1", "eps1", "root1", "normed1"))
        bn2, stats2, eps2, root2, normed2 = (sem(n) for n in ("bn2", "stats2", "eps2", "root2", "normed2"))
        q_hi, k_hi = sem("q_hi"), sem("k_hi")
        k_blocks, q_blocks, q_blocks_more = sem("k_blocks"), sem("q_blocks"), sem("q_blocks_more")
        s_made, s_maxed = sem("s_made"), sem("s_maxed")
        p_made, exp_done = sem("p_made"), sem("exp_done")
        pv_made, o_inverted, o_normed = sem("pv_made"), sem("o_inverted"), sem("o_normed")

        block = ctx.enter_context(nc.Block())

        def steps(engine, step):
            for t in range(-LOAD, FIRST):
                step(Band(None, t))
            with engine.Fori(0, rounds) as i:
                for t in range(BANDS):
                    step(Band(i, FIRST + t))
            for t in range(FIRST + BANDS * rounds, NB - RESULT[1]):
                step(Band(None, t))

        def has(b):
            return b.i is not None or 0 <= b.c < NB

        def wait(engine, s, value):
            if not isinstance(value, int) or value > 0:
                engine.wait_ge(s, value)

        def alone(engine):
            engine.sem_inc(passed, 1)

        def bank(t, name):
            return G_BANK + BANK[t.c % 2][name]

        def after(b, name):
            return b.used(2, 1) if name in PAIRED else b.count(TAKES[name], TAKES[name])

        def query_chunk(u, n):
            return 2 * (u % 2) + n, u // 2

        def made_count(b, name):
            return b.used(2, 1) if name in PAIRED else b.count(1, 1)

        def chunk(u, n):
            return divmod(2 * u + n, QUADS)

        def image_rows(c):
            r = (c % BANDS) * WS + SHIFT
            return [(0, r, WS - SHIFT), (WS - SHIFT, (r + WS - SHIFT) % SIDE, SHIFT)]

        @block.sync
        def _(sp):
            def const(dst, src):
                sp.dma_start(dst, src).then_inc(consts_in, 16)

            def column(n, v):
                const(vec[:, n:n + 1], v.rearrange("(c a) -> c a", a=1))

            sp.wait_ge(filled, 1)
            const(ident[:, :], ident_d)
            const(heads[:, :], heads_d)
            const(wraw[:, :], wqkv)
            const(w1raw[:, :], wfc1)
            const(wp[0:C, :], wproj)
            for m in range(2):
                const(w2[0:C, m, :], wfc2[m * C:(m + 1) * C, :])
                column(BF1 + m, bfc1[m * C:(m + 1) * C])
            const(w2[C:C + 1, 0, :], bfc2.rearrange("(a c) -> a c", a=1))
            for m in range(3):
                column(BQ + m, bqkv[m * C:(m + 1) * C])
            for n, v in ((G1, g1), (B1, b1), (BP, bproj), (G2, g2), (B2, b2)):
                column(n, v)
            const(regions[:, :, :, :], rows_d[:, :, 0:4, 0, :].rearrange("n k r t -> r n k t"))
            for n in range(4):
                const(qst[MASK0:ROWS, n, :, :], rows_d[0, 0, :, :, :])
                const(kst[MASK0:ROWS, n, :, :], rows_d[1, 0, :, :, :])
            sp.wait_ge(consts_in, 16 * N_CONST)

            def load_x(b):
                n = b.c % 4
                wait(sp, x_ordered, b.count(1, -3))
                alone(sp)
                for at, row, rows in image_rows(b.c):
                    sp.dma_start(xr[:, n, at:at + rows, :], x[b.image(), :, row:row + rows, :]).then_inc(x_in[n], 16)

            def stacks(b):
                n = b.c % 4
                wait(sp, p_made, b.count(UNITS, -3 * UNITS))
                alone(sp)
                if n == 3:
                    kind = int(b.c % BANDS == BANDS - 1)
                    sp.dma_start(qst[MASK0:MAX0, n, :, :], rows_d[0, kind, 0:4, :, :]).then_inc(stack_in[n], 16)
                    sp.dma_start(kst[MASK0:MAX0, n, :, :], rows_d[1, kind, 0:4, :, :]).then_inc(stack_in[n], 16)
                sp.wait_ge(nat_out[n], b.used(4, 16))
                alone(sp)
                src = nat_d[n, :, :, :].rearrange("(c r) n t -> n r c t", c=QUADS)
                for stack, parts in ((kst, (2, 3, 2)), (qst, (0, 0, 1))):
                    for m, part in enumerate(parts):
                        sp.dma_start(stack[32 * m:32 * m + 32, n, :, :], src[part, :, :, :]).then_inc(stack_in[n], 16)

            def maxima(b):
                n = b.c % 2
                wait(sp, max_in[n], b.step(-2).used(2, QUADS * 16))
                alone(sp)
                sp.wait_ge(taken["mt"], b.count(1, 1))
                alone(sp)
                sp.dma_start(max_d[n, :, :, :].rearrange("p h t -> (p h) t"), mrow[:, n, :]).then_inc(max_out[n], 16)
                sp.wait_ge(max_out[n], b.used(2, 16))
                alone(sp)
                for c in range(QUADS):
                    sp.dma_start(qst[MAX0:ROWS, b.c % 4, c, :].rearrange("h (p t) -> h p t", t=PT),
                                 max_d[n, :, 4 * c:4 * c + 4, :].rearrange("p h t -> h p t")).then_inc(max_in[n], 16)

            def save_parts(b):
                n = b.c % 4
                wait(sp, stack_in[n], b.step(-4).used(4, STACK_IN[n]))
                alone(sp)
                sp.wait_ge(taken["q"], b.count(1, 1))
                alone(sp)
                sp.wait_ge(taken["k"], b.count(1, 1))
                alone(sp)
                sp.dma_start(nat_d[n, :, :, :], nat[:, n, :, :]).then_inc(nat_out[n], 16)

            def store_y(b):
                n = b.c % 2
                sp.wait_ge(taken[f"fc2{n}"], b.used(2, 1))
                alone(sp)
                for at, row, rows in image_rows(b.c):
                    sp.dma_start(out[b.image(), :, row:row + rows, :], yr[:, n, at:at + rows, :]).then_inc(y_out[n], 16)

            def step(t):
                for offset, stage in ((LOAD, load_x), (STACK, stacks), (MAXIMA, maxima), (QK, save_parts)):
                    if has(t.step(offset)):
                        stage(t.step(offset))
                for offset in RESULT:
                    if t.c % 2 == 0 and has(t.step(offset)):
                        store_y(t.step(offset))

            steps(sp, step)
            for n in range(2):
                sp.wait_ge(y_out[n], 2 * 16 * NB // 2)

        @block.gpsimd
        def _(pool):
            nc.gpsimd.memset(half[:, :], -0.5)
            nc.gpsimd.memset(vbd[:, :, :, :, :], 0.0).then_inc(vbd_zero, 1)
            pool.wait_ge(vbd_zero, 1)
            nc.gpsimd.memset(vbd[0:L, :, :, 0, HD:HD + 1], 1.0)
            nc.gpsimd.memset(vbd[W1:PR, :, :, 1, HD:HD + 1], 1.0).then_inc(vbd_ones, 1)
            pool.wait_ge(vbd_ones, 1)
            pool.wait_ge(consts_in, 16 * N_CONST)

            def order_x(b):
                pool.wait_ge(x_in[b.c % 4], b.used(4, 2 * 16))
                alone(pool)
                wait(pool, taken["proj"], b.count(1, -7))
                alone(pool)
                src, dst, inner = xr[:, b.c % 4, :, :], xw[:, b.c % 8, :], BANDS - 1
                nc.gpsimd.tensor_copy(dst[:, 0:inner * L].rearrange("c (w r s) -> c w r s", w=inner, r=WS),
                                      src[:, :, SHIFT:SHIFT + inner * WS].rearrange("c r (w s) -> c w r s", s=WS))
                end = dst[:, inner * L:TOK].rearrange("c (r s) -> c r s", r=WS)
                nc.gpsimd.tensor_copy(end[:, :, 0:WS - SHIFT], src[:, :, SIDE - WS + SHIFT:SIDE])
                nc.gpsimd.tensor_copy(end[:, :, WS - SHIFT:WS], src[:, :, 0:SHIFT]).then_inc(x_ordered, 1)

            def root(b, mv, ve, rs, stats, eps, done):
                n = b.c % 2
                pool.wait_ge(stats, b.count(1, 1))
                alone(pool)
                nc.gpsimd.tensor_scalar(ve[:, n, :], mv[:, n, :, 1], EPS, None, ALU.add).then_inc(eps, 1)
                pool.wait_ge(eps, b.count(1, 1))
                alone(pool)
                nc.gpsimd.tensor_tensor(rs[:, n, :], ve[:, n, :], half[0:PT, :], ALU.pow).then_inc(done, 1)

            def normalise(b, root, transposed, tok, mv, rs, xn, done):
                n = b.c % 2
                pool.wait_ge(root, b.count(1, 1))
                alone(pool)
                wait(pool, transposed, b.count(1, -1))
                alone(pool)
                for p in range(PAIRS):
                    last = nc.gpsimd.tensor_scalar(xn[:, n, p, :], tok[:, n, p, :], mv[:, n, p, 0:1], rs[:, n, p:p + 1], ALU.subtract, ALU.mult)
                last.then_inc(done, 1)

            def step(t):
                if has(t.step(TOKENS)):
                    root(t.step(TOKENS), mv1, ve1, rs1, stats1, eps1, root1)
                    normalise(t.step(TOKENS), root1, made["t2"], tok1, mv1, rs1, xn1, normed1)
                if has(t.step(ORDER)):
                    order_x(t.step(ORDER))
                if has(t.step(PROJ)):
                    root(t.step(PROJ), mv2, ve2, rs2, stats2, eps2, root2)

            steps(pool, step)

        @block.tensor
        def _(pe):
            pe.wait_ge(consts_in, 16 * N_CONST)
            pe.wait_ge(psum_clear, 1)
            pe.wait_ge(hid_one, 1)
            for n in range(3):
                nc.tensor.matmul(psum[0:C, 0, n:n + 1], wraw[:, n * C:(n + 1) * C], vec[:, B1:B1 + 1], start=True, stop=True)
            for n in range(2):
                last = nc.tensor.matmul(psum[0:C, 0, 3 + n:4 + n], w1raw[:, n * C:(n + 1) * C], vec[:, B2:B2 + 1], start=True, stop=True)
            last.then_inc(bias_made, 1)
            pe.wait_ge(bias_set, 1)
            nc.tensor.matmul(psum[0:C, 0, 5:6], wp[0:C, :], bias[:, 2:3], start=True, stop=True).then_inc(bias_made, 1)
            pe.wait_ge(bias_set, 2)
            pe.wait_ge(weights_set, 1)
            pe.wait_ge(vbd_ones, 1)

            def general(t, name):
                at = t.c * len(ORDERED) + ORDERED.index(name)
                while at > -LOAD * len(ORDERED):
                    at -= 1
                    c, n = divmod(at, len(ORDERED))
                    last = ORDERED[n]
                    before = Band(t.i, c + GENERAL[last])
                    if BANK[c % 2].get(last) == BANK[t.c % 2][name] and has(before):
                        pe.wait_ge(taken[last], after(before, last))
                        break
                return psum[:, bank(t, name), :]

            def transposes(t, name, ready, src, rows):
                b = t.step(GENERAL[name])
                if not has(b):
                    return
                pe.wait_ge(ready, b.count(1, 1))
                dst = general(t, name)
                for p in range(PAIRS):
                    part = src(b, p)
                    other = PT + C - rows
                    last = nc.tensor.transpose(dst[0:other, p * rows:(p + 1) * rows], part, ident[0:rows, 0:rows])
                last.then_inc(made[name], 1)

            def dense(t, name, ready, parts):
                b = t.step(GENERAL[name])
                if not has(b) or name not in BANK[t.c % 2]:
                    return
                pe.wait_ge(taken[ready], after(b, ready))
                dst = general(t, name)
                parts = parts(b)
                for n, (weights, tokens) in enumerate(parts):
                    last = nc.tensor.matmul(dst[0:C, 0:TOK], weights, tokens, start=n == 0, stop=n == len(parts) - 1)
                last.then_inc(made[name], 1)

            def values(t):
                b = t.step(STACK)
                if not has(b):
                    return
                dst = general(t, "v")
                for p in range(PAIRS):
                    for w in range(2):
                        at = (2 * p + w) * L
                        last = nc.tensor.matmul(dst[W1 * w:W1 * w + L, p * C:(p + 1) * C], xnT[:, b.c % 4, at:at + L], wv[:, :], start=True, stop=True)
                last.then_inc(made["v"], 1)

            def out_transposes(t):
                b = t.step(PROJ)
                if not has(b):
                    return
                pe.wait_ge(o_normed, b.count(2, 2))
                dst = general(t, "ot")
                alone(pe)
                for d in range(2):
                    for w in range(2):
                        n = 2 * d + w
                        last = nc.tensor.transpose(dst[0:C, n * 2 * W1:n * 2 * W1 + PR], on[:, b.c % 2, d, w, :], ident[0:PR, 0:PR])
                last.then_inc(made["ot"], 1)

            def max_transpose(t):
                b = t.step(MAXIMA)
                if not has(b):
                    return
                pe.wait_ge(s_maxed, b.count(UNITS, UNITS))
                dst = general(t, "mt")
                alone(pe)
                nc.tensor.transpose(dst[0:PAIRS * NH, 0:PR], nmax[:, b.c % 2, :], ident[0:PR, 0:PR]).then_inc(made["mt"], 1)

            def scores(t, u):
                b = t.step(SCORE)
                if not has(b):
                    return
                if u == 0:
                    pe.wait_ge(k_blocks, b.count(1, 1))
                wait(pe, s_maxed, b.count(UNITS, u - 1))
                kind = int(b.c % BANDS == BANDS - 1)
                for n in range(2):
                    p, c = query_chunk(u, n)
                    for w in range(2):
                        window = 2 * p + w
                        masked = kind == 1 or window == BANDS - 1
                        toks = slice(window * L, (window + 1) * L)
                        dst = psum[W1 * w:W1 * w + L, S_BANK + u % 2, n * CH:(n + 1) * CH]
                        last = nc.tensor.matmul(dst, qsd[:, b.c % 2, c, toks], kbd[:, b.c % 2, :, toks],
                                                start=True, stop=not masked)
                        if masked:
                            keys = regions[:, 1, kind, toks].rearrange("r (h t) -> r h t", h=1).to_broadcast([4, 4, L])
                            last = nc.tensor.matmul(dst, regions[:, 0, kind, toks], keys, start=False, stop=True)
                last.then_inc(s_made, 1)

            def shifted(t, u):
                b = t.step(PROB)
                if not has(b):
                    return
                if u == 0:
                    pe.wait_ge(q_blocks, b.count(1, 1))
                    pe.wait_ge(q_blocks_more, b.count(2, 2))
                wait(pe, exp_done, b.count(UNITS, u - 1))
                for n in range(2):
                    p, c = chunk(u, n)
                    for w in range(2):
                        toks = slice((2 * p + w) * L, (2 * p + w + 1) * L)
                        last = nc.tensor.matmul(psum[W1 * w:W1 * w + L, P_BANK + u % 2, n * CH:(n + 1) * CH], kst[:, b.c % 4, c, toks], qbd[:, b.c % 2, c, :, toks],
                                                start=True, stop=True)
                last.then_inc(p_made, 1)

            def weighted(t, d):
                b = t.step(PROB if d == 0 else PROJ)
                if not has(b):
                    return
                if d == 0:
                    pe.wait_ge(taken["v"], b.count(2, 2))
                pe.wait_ge(exp_done, b.count(UNITS, UNITS // 2 * (d + 1)))
                wait(pe, o_normed, b.count(2, d))
                for h in range(NH):
                    for n in range(2):
                        p = 2 * d + n
                        dst = psum[W1 * n:W1 * n + L, O_BANK, O_HALF * d:O_HALF * d + 2 * NH * (HD + 1)].rearrange("t (w h e) -> t w h e", w=2, h=NH)
                        last = nc.tensor.matmul(dst[:, :, h, :], probs[:, b.c % 2, p * QUADS + h // 4, h % 4 * L:(h % 4 + 1) * L],
                                                vbd[:, b.c % 4, p * NH + h, :, :], start=True, stop=True)
                last.then_inc(pv_made, 1)

            def fc1(m):
                return lambda b: [(w1[:, m * C:(m + 1) * C], fnT[:, b.c % 2, :])]

            def fc2(b):
                return [(w2[:, m, :], hid[:, b.c % 2, m, :]) for m in range(2)]

            def step(t):
                shifted(t, 0)
                transposes(t, "t2", normed1, lambda b, p: xn1[:, b.c % 2, p, :], PT)
                weighted(t, 1)
                scores(t, 0)
                shifted(t, 1)
                transposes(t, "t1", x_ordered, lambda b, p: xw[:, b.c % 8, p * PT:(p + 1) * PT], C)
                max_transpose(t)
                scores(t, 1)
                shifted(t, 2)
                dense(t, "q", "t2", lambda b: [(wq[:, :], xnT[:, b.c % 4, :])])
                out_transposes(t)
                scores(t, 2)
                shifted(t, 3)
                transposes(t, "nt2", normed2, lambda b, p: xn2[:, b.c % 2, p, :], PT)
                shifted(t, 4)
                dense(t, "k", "t2", lambda b: [(wk[:, :], xnT[:, b.c % 4, :])])
                scores(t, 3)
                dense(t, "proj", "ot", lambda b: [(wp[:, :], oT[:, b.c % 2, :])])
                dense(t, "fca0", "nt2", fc1(0))
                dense(t, "fcb0", "nt2", fc1(1))
                dense(t, "fca1", "nt2", fc1(0))
                dense(t, "fc20", "fcb0", fc2)
                dense(t, "fcb1", "nt2", fc1(1))
                weighted(t, 0)
                scores(t, 4)
                shifted(t, 5)
                transposes(t, "nt1", taken["proj"], lambda b, p: f[:, b.c % 4, p * PT:(p + 1) * PT], C)
                values(t)
                scores(t, 5)
                dense(t, "fc21", "fcb1", fc2)

            steps(pe, step)

        @block.scalar
        def _(act):
            act.wait_ge(bias_set, 2)
            act.wait_ge(vbd_ones, 1)

            def product(t, name):
                b = t.step(GENERAL[name])
                act.wait_ge(made[name], made_count(b, name))
                return b, psum[:, bank(t, name), :]

            def out_by_channel(t):
                b, src = product(t, "ot")
                wait(act, made["proj"], b.count(1, -1))
                for d in range(2):
                    nc.scalar.activation(oT[0:C, b.c % 2, d * 2 * PT:(d + 1) * 2 * PT].rearrange("c (p w t) -> c p w t", p=2, w=2),
                                         src[0:C, d * 4 * W1:(d + 1) * 4 * W1].rearrange("c (w p t) -> c p w t", w=2, p=2)[:, :, :, 0:L],
                                         ACT.Copy).then_inc(taken["ot"], 1)

            def max_rows(t):
                b, src = product(t, "mt")
                wait(act, max_out[b.c % 2], b.step(-2).used(2, 16))
                nc.scalar.activation(mrow[:, b.c % 2, :].rearrange("h (w t) -> h w t", w=2),
                                     src[0:PAIRS * NH, 0:2 * W1].rearrange("h (w t) -> h w t", w=2)[:, :, 0:L],
                                     ACT.Copy).then_inc(taken["mt"], 1)

            def x_by_channel(t):
                b, src = product(t, "t2")
                wait(act, made["v"], b.count(1, -3))
                nc.scalar.activation(xnT[0:C, b.c % 4, :], src[0:C, 0:TOK], ACT.Copy).then_inc(taken["t2"], 1)

            def x_by_token(t):
                b, src = product(t, "t1")
                wait(act, normed1, b.count(1, -1))
                nc.scalar.activation(tok1[:, b.c % 2, :, :], src[0:PT, 0:PAIRS * C].rearrange("t (p c) -> t p c", c=C), ACT.Copy).then_inc(taken["t1"], 1)

            def f_by_channel(t):
                b, src = product(t, "nt2")
                wait(act, made[f"fcb{b.c % 2}"], b.step(-2).used(2, 1))
                nc.scalar.activation(fnT[0:C, b.c % 2, :], src[0:C, 0:TOK], ACT.Copy).then_inc(taken["nt2"], 1)

            def f_by_token(t):
                b, src = product(t, "nt1")
                wait(act, normed2, b.count(1, -1))
                nc.scalar.activation(tok2[:, b.c % 2, :, :], src[0:PT, 0:PAIRS * C].rearrange("t (p c) -> t p c", c=C), ACT.Copy).then_inc(taken["nt1"], 1)

            def high_part(t, name, part, col, done):
                b, src = product(t, name)
                if name == "q":
                    wait(act, nat_out[b.c % 4], b.step(-4).used(4, 16))
                    wait(act, k_blocks, b.count(1, -3))
                nc.scalar.activation(nat[:, b.c % 4, part, :], src[0:C, 0:TOK], ACT.Identity, bias=bias[:, col:col + 1]).then_inc(done, 1)

            def value_blocks(t):
                b, src = product(t, "v")
                wait(act, pv_made, b.count(2, -6))
                for w in range(2):
                    rows = slice(W1 * w, W1 * w + L)
                    nc.scalar.activation(vbd[rows, b.c % 4, :, w, 0:HD], src[rows, 0:PAIRS * C].rearrange("t (h d) -> t h d", d=HD),
                                         ACT.Copy).then_inc(taken["v"], 1)

            def exps(t, u):
                b = t.step(PROB)
                if has(b):
                    act.wait_ge(p_made, b.count(UNITS, u + 1))
                    if u == 0:
                        wait(act, pv_made, b.count(2, -2))
                    nc.scalar.activation(probs[0:PR, b.c % 2, 2 * u:2 * u + 2, :], psum[0:PR, P_BANK + u % 2, 0:2 * CH].rearrange("j (n k) -> j n k", n=2),
                                         ACT.Exp).then_inc(exp_done, 1)

            def block_q_more(t, h):
                b = t.step(QBLOCK)
                if h == 2:
                    act.wait_ge(stack_in[b.c % 4], b.used(4, STACK_IN[b.c % 4]))
                    act.wait_ge(max_in[b.c % 2], b.used(2, QUADS * 16))
                    wait(act, p_made, b.count(UNITS, -UNITS))
                nc.scalar.activation(qbd[0:ROWS, b.c % 2, :, h, :], qst[0:ROWS, b.c % 4, :, :], ACT.Copy, scale=heads[:, h:h + 1]).then_inc(q_blocks_more, 1)

            def gelu(t, n, m):
                name = ("fca", "fcb")[m] + str(n)
                if t.c % 2 == 0 or not has(t.step(HIDDEN[n])):
                    return
                b, src = product(t, name)
                if m == 0:
                    wait(act, made[f"fc2{n}"], b.step(-2).used(2, 1))
                nc.scalar.activation(hid[0:C, n, m, :], src[0:C, 0:TOK], ACT.Gelu, bias=bias[:, 3 + m:4 + m]).then_inc(taken[name], 1)

            def step(t):
                def run(offset, stage, *more):
                    if has(t.step(offset)):
                        stage(t, *more)

                exps(t, 0)
                run(QK, x_by_channel)
                run(QBLOCK, block_q_more, 2)
                run(TOKENS, x_by_token)
                run(MAXIMA, max_rows)
                exps(t, 1)
                run(QK, high_part, "q", 0, 0, q_hi)
                run(PROJ, out_by_channel)
                exps(t, 2)
                run(QBLOCK, block_q_more, 3)
                run(NORM2, f_by_channel)
                run(QK, high_part, "k", 2, 1, k_hi)
                exps(t, 3)
                gelu(t, 0, 0)
                gelu(t, 0, 1)
                gelu(t, 1, 0)
                gelu(t, 1, 1)
                exps(t, 4)
                exps(t, 5)
                run(PROJ, f_by_token)
                run(STACK, value_blocks)

            steps(act, step)

        @block.vector
        def _(dve):
            for a in (wq, wk, wv, wp, w1, w2, xnT, fnT, oT, hid, qst, kst, qbd, kbd, qsd, probs):
                last = nc.vector.memset(a[FILL:FULL], 0.0)
            last.then_inc(filled, 1)
            dve.wait_ge(filled, 1)
            nc.vector.memset(hid[C:C + 1, :, 0, :], 1.0).then_inc(hid_one, 1)
            nc.vector.memset(psum[:, :, :], 1.0).then_inc(psum_clear, 1)
            dve.wait_ge(consts_in, 16 * N_CONST)
            g = vec[:, G1:G1 + 1]
            nc.vector.tensor_scalar(wq[0:C, :], wraw[:, 0:C], g, SCALE, ALU.mult, ALU.mult)
            nc.vector.tensor_scalar(wk[0:C, :], wraw[:, C:2 * C], g, None, ALU.mult)
            nc.vector.tensor_scalar(wv[0:C, :], wraw[:, 2 * C:3 * C], g, None, ALU.mult)
            nc.vector.tensor_scalar(w1[0:C, :], w1raw[:, :], vec[:, G2:G2 + 1], None, ALU.mult).then_inc(weights_set, 1)
            dve.wait_ge(bias_made, 1)
            nc.vector.tensor_scalar(bias[:, 0:1], psum[0:C, 0, 0:1], vec[:, BQ:BQ + 1], SCALE, ALU.add, ALU.mult)
            for n, raw in ((1, BK), (3, BF1), (4, BF1 + 1), (2, BV)):
                last = nc.vector.tensor_tensor(bias[:, n:n + 1], psum[0:C, 0, n:n + 1], vec[:, raw:raw + 1], ALU.add)
            last.then_inc(bias_set, 1)
            dve.wait_ge(bias_made, 2)
            nc.vector.tensor_tensor(bias[:, 5:6], psum[0:C, 0, 5:6], vec[:, BP:BP + 1], ALU.add).then_inc(bias_set, 1)
            dve.wait_ge(bias_set, 2)

            def product(t, name):
                b = t.step(GENERAL[name])
                dve.wait_ge(made[name], made_count(b, name))
                return b, psum[:, bank(t, name), :]

            def stats(b, by_token, tok, st, mv, bn, done):
                n = b.c % 2
                dve.wait_ge(by_token, b.count(1, 1))
                for p in range(PAIRS):
                    last = nc.vector.bn_stats(st[:, n, p, :], tok[:, n, p, :])
                last.then_inc(bn, 1)
                dve.wait_ge(bn, b.count(1, 1))
                alone(dve)
                for p in range(PAIRS):
                    last = nc.vector.bn_aggr(mv[:, n, p, :], st[:, n, p, :])
                last.then_inc(done, 1)

            def normalise(b, root, transposed, tok, mv, rs, xn, done):
                n = b.c % 2
                dve.wait_ge(root, b.count(1, 1))
                wait(dve, transposed, b.count(1, -1))
                for p in range(PAIRS):
                    last = nc.vector.tensor_scalar(xn[:, n, p, :], tok[:, n, p, :], mv[:, n, p, 0:1], rs[:, n, p:p + 1], ALU.subtract, ALU.mult)
                last.then_inc(done, 1)

            def maxima(t, u):
                b = t.step(SCORE)
                if has(b):
                    dve.wait_ge(s_made, b.count(UNITS, u + 1))
                    if u == 0:
                        wait(dve, made["mt"], b.count(1, -1))
                    p, c = query_chunk(u, 0)
                    dst = nmax[:, b.c % 2, :].rearrange("i (p h) -> i p h", h=NH)[:, p:p + 2, 4 * c:4 * c + 4]
                    nc.vector.tensor_reduce(dst, psum[0:PR, S_BANK + u % 2, 0:2 * CH].rearrange("i (p h j) -> i p h j", p=2, j=L),
                                            axis=AX.X, op=ALU.max, negate=True).then_inc(s_maxed, 1)

            def residual(t):
                b, src = product(t, "proj")
                wait(dve, taken[f"fc2{b.c % 2}"], b.step(-4).used(2, 1))
                wait(dve, made["nt1"], b.count(1, -3))
                nc.vector.scalar_tensor_tensor(out=f[:, b.c % 4, :], in0=src[0:C, 0:TOK], scalar=bias[:, 5:6], in1=xw[:, b.c % 8, :],
                                               op0=ALU.add, op1=ALU.add).then_inc(taken["proj"], 1)

            def low_part(t, name, part, col, high):
                b, src = product(t, name)
                n = b.c % 4
                dve.wait_ge(high, b.count(1, 1))
                nc.vector.scalar_tensor_tensor(out=nat[:, n, part + 1, :], in0=src[0:C, 0:TOK], scalar=bias[:, col:col + 1], in1=nat[:, n, part, :],
                                               op0=ALU.add, op1=ALU.subtract).then_inc(taken[name], 1)

            def block_k(t):
                b = t.step(KBLOCK)
                if not has(b):
                    return
                dve.wait_ge(k_hi, b.count(1, 1))
                wait(dve, s_made, b.count(UNITS, -UNITS))
                for h in range(4):
                    last = nc.vector.tensor_scalar(kbd[0:C, b.c % 2, h, :], nat[:, b.c % 4, 2, :], heads[0:C, h:h + 1], None, ALU.mult)
                for c in range(QUADS):
                    last = nc.vector.tensor_scalar(qsd[0:C, b.c % 2, c, :], nat[:, b.c % 4, 0, :], heads[0:C, 4 + c:5 + c], None, ALU.mult)
                last.then_inc(k_blocks, 1)

            def block_q(t):
                b = t.step(QBLOCK)
                if not has(b):
                    return
                dve.wait_ge(stack_in[b.c % 4], b.used(4, STACK_IN[b.c % 4]))
                dve.wait_ge(max_in[b.c % 2], b.used(2, QUADS * 16))
                wait(dve, p_made, b.count(UNITS, -UNITS))
                for h in range(2):
                    last = nc.vector.tensor_scalar(qbd[0:ROWS, b.c % 2, :, h, :], qst[0:ROWS, b.c % 4, :, :], heads[:, h:h + 1], None, ALU.mult)
                last.then_inc(q_blocks, 1)

            def divide(t, d):
                b = t.step(PROB if d == 0 else PROJ)
                if not has(b):
                    return
                dve.wait_ge(pv_made, b.count(2, d + 1))
                src = psum[0:PR, O_BANK, O_HALF * d:O_HALF * d + 2 * NH * (HD + 1)].rearrange("t (n e) -> t n e", e=HD + 1)
                nc.vector.reciprocal(rsum[:, d, :].rearrange("t (n e) -> t n e", e=1), src[:, :, HD:HD + 1]).then_inc(o_inverted, 1)
                dve.wait_ge(o_inverted, b.count(2, d + 1))
                if d == 0:
                    wait(dve, made["ot"], b.count(1, -1))
                nc.vector.tensor_tensor(on[:, b.c % 2, d, :, :].rearrange("t w (h e) -> t (w h) e", e=HD), src[:, :, 0:HD],
                                        rsum[:, d, :].rearrange("t (n e) -> t n e", e=1).to_broadcast([PR, 2 * NH, HD]), ALU.mult).then_inc(o_normed, 1)

            def result(t, n):
                if t.c % 2 == 1 or not has(t.step(RESULT[n])):
                    return
                b, src = product(t, f"fc2{n}")
                wait(dve, y_out[b.c % 2], b.step(-2).used(2, 2 * 16))
                dst, res, inner = yr[:, b.c % 2, :, :], f[:, b.c % 4, :], BANDS - 1
                parts = [(dst[:, :, SHIFT:SHIFT + inner * WS].rearrange("c r (w s) -> c w r s", s=WS),
                          *(v[:, 0:inner * L].rearrange("c (w r s) -> c w r s", w=inner, r=WS) for v in (src[0:C, :], res)))]
                ends = [v[:, inner * L:TOK].rearrange("c (r s) -> c r s", r=WS) for v in (src[0:C, :], res)]
                parts.append((dst[:, :, SIDE - WS + SHIFT:SIDE], *(v[:, :, 0:WS - SHIFT] for v in ends)))
                parts.append((dst[:, :, 0:SHIFT], *(v[:, :, WS - SHIFT:WS] for v in ends)))
                for to, a, c in parts:
                    last = nc.vector.tensor_tensor(to, a, c, ALU.add)
                last.then_inc(taken[f"fc2{n}"], 1)

            def step(t):
                def run(offset, stage, *more):
                    if has(t.step(offset)):
                        stage(t, *more)

                divide(t, 1)
                maxima(t, 0)
                maxima(t, 1)
                if has(t.step(NORM2)):
                    normalise(t.step(NORM2), root2, made["nt2"], tok2, mv2, rs2, xn2, normed2)
                run(QK, low_part, "q", 0, 0, q_hi)
                if has(t.step(TOKENS)):
                    stats(t.step(TOKENS), taken["t1"], tok1, st1, mv1, bn1, stats1)
                maxima(t, 2)
                maxima(t, 3)
                run(QK, low_part, "k", 2, 1, k_hi)
                run(PROJ, residual)
                block_k(t)
                result(t, 0)
                block_q(t)
                divide(t, 0)
                maxima(t, 4)
                maxima(t, 5)
                result(t, 1)
                if has(t.step(PROJ)):
                    stats(t.step(PROJ), taken["nt1"], tok2, st2, mv2, bn2, stats2)

            steps(dve, step)


def constants():
    ident = np.eye(128, dtype=np.float32)
    heads = np.zeros((ROWS, 7), np.float32)
    for h in range(NH):
        heads[HD * h:HD * (h + 1), 4 + h // 4] = 1
    for h in range(4):
        for part in range(3):
            heads[32 * part + HD * h:32 * part + HD * h + HD, h] = 1
        heads[MASK0:MAX0, h] = 1
        heads[MAX0 + h, h] = 1
    rows = np.zeros((2, 2, 8, QUADS, TOK), np.float16)
    for kind in range(2):
        for w in range(BANDS):
            for r in range(WS):
                for s in range(WS):
                    lower = kind == 1 and r >= WS - SHIFT
                    right = w == BANDS - 1 and s >= WS - SHIFT
                    region = 2 * lower + right
                    t = w * L + r * WS + s
                    rows[0, kind, 0:4, :, t] = -100
                    rows[0, kind, region, :, t] = 0
                    rows[1, kind, region, :, t] = 1
        rows[1, kind, 4:8] = 1
    return ident, heads, rows


_INS = ["x"] + ["L0_conv_" + n for n in ("g1", "b1", "w_qkv", "b_qkv", "w_proj", "b_proj", "g2", "b2", "w_fc1", "b_fc1", "w_fc2", "b_fc2")]


def kernel(**inputs):
    import concourse.bacc as _bacc
    from concourse.bass_utils import run_bass_kernel_spmd as _run

    nc = _bacc.Bacc("TRN2", target_bir_lowering=False, num_devices=1)
    given = {n: np.ascontiguousarray(inputs[n]) for n in _INS}
    given |= dict(zip(("ident", "heads", "rows"), constants()))
    arrays, args = {}, []
    for name, a in given.items():
        arrays[f"in_{name}_dram"] = a
        args.append(nc.dram_tensor(f"in_{name}_dram", a.shape, mybir.dt.from_np(a.dtype), kind="ExternalInput").ap())
    args.append(nc.dram_tensor("out_0_dram", given["x"].shape, F32, kind="ExternalOutput").ap())
    build(nc, *args)
    r = _run(nc, [arrays], core_ids=[0])
    return r.results[0]["out_0_dram"]
```
